# Optimizing a Trainium2 kernel written in Bass

```python
import numpy as np
import jax
import jax.numpy as jnp

def _softmax(x, axis=-1):
    return jax.nn.softmax(x, axis=axis)

def _gelu(x):
    return jax.nn.gelu(x, approximate=True)

def _silu(x):
    return jax.nn.silu(x)

def _sigmoid(x):
    return jax.nn.sigmoid(x)

def _layernorm(x, axis=-1, eps=1e-05):
    m = jnp.mean(x, axis=axis, keepdims=True)
    v = jnp.var(x, axis=axis, keepdims=True)
    return (x - m) / jnp.sqrt(v + eps)

def _scatter_add(tgt, idx, src, axis=0):
    return tgt.at[idx].add(src)

def _segment_sum(src, seg, n):
    return jax.ops.segment_sum(src, seg, n)
kernel_name = 'mk_adj_ffn_d1_adj_r2_e8e964'

def setup_inputs(seed: int=0):
    np.random.seed(seed)
    _w = jnp.asarray

    def _rec_inputs():
        import jax
        import jax.numpy as jnp
        _gk = jax.random.key(seed)
        x = -0.0002928 + 1 * jax.random.normal(jax.random.fold_in(_gk, 1), (32, 256, 128), jnp.float32)
        _a = jax.random.bernoulli(jax.random.fold_in(_gk, 2), 0.0625, (32, 256, 256))
        _af = _a.astype(jnp.float32)
        adj = _af
        _nm = jnp.ones((32, 256), dtype=bool)
        nodemask = jnp.where(_nm, 1.0, 0.0).astype(jnp.float32)
        return (x, adj, nodemask)
    x, adj, nodemask = _rec_inputs()

    def _L0_gnn_setup():
        import jax, jax.numpy as jnp
        import numpy as np
        B, N, IN_DIM, OUT_DIM = (8, 1024, 128, 128)
        EDGE_P = 0.02
        MASK_P = 0.9
        key = jax.random.key(seed)
        ks = jax.random.split(key, 8)
        x = jax.random.normal(ks[0], (B, N, IN_DIM), dtype=jnp.float32)
        adj = (jax.random.uniform(ks[1], (B, N, N)) < EDGE_P).astype(jnp.float32)
        mask = (jax.random.uniform(ks[2], (B, N)) < MASK_P).astype(jnp.float32)
        lim1 = 1.0 / np.sqrt(IN_DIM)
        W = jax.random.uniform(ks[3], (OUT_DIM, IN_DIM), minval=-lim1, maxval=lim1, dtype=jnp.float32)
        b = jax.random.uniform(ks[4], (OUT_DIM,), minval=-lim1, maxval=lim1, dtype=jnp.float32)
        lim2 = 1.0 / np.sqrt(2 * OUT_DIM)
        a1 = jax.random.uniform(ks[5], (OUT_DIM,), minval=-lim2, maxval=lim2, dtype=jnp.float32)
        a2 = jax.random.uniform(ks[6], (OUT_DIM,), minval=-lim2, maxval=lim2, dtype=jnp.float32)
        att_b = jax.random.uniform(ks[7], (), minval=-lim2, maxval=lim2, dtype=jnp.float32)
        return {'x': x, 'adj': adj, 'mask': mask, 'W': W, 'b': b, 'a1': a1, 'a2': a2, 'att_b': att_b}
    _L0_gnn_all = _L0_gnn_setup()
    _L0_gnn_in = {k: v for k, v in _L0_gnn_all.items() if k in ('W', 'b', 'a1', 'a2', 'att_b')}
    del _L0_gnn_all

    def _L0_ffn_setup():
        import jax, jax.numpy as jnp
        import numpy as np
        B, S, H, F, E, K = (8, 2048, 128, 256, 16, 2)
        EPS = 1e-05
        key = jax.random.key(seed)
        ks = jax.random.split(key, 9)
        sc = 0.02
        return {'x': jax.random.normal(ks[0], (B, S, H), dtype=jnp.float32), 'gate_w': jax.random.normal(ks[1], (H, E), dtype=jnp.float32) * sc, 'gate_b': jnp.zeros((E,), dtype=jnp.float32), 'w1': jax.random.normal(ks[2], (E, H, F), dtype=jnp.float32) * sc, 'b1': jnp.zeros((E, F), dtype=jnp.float32), 'w2': jax.random.normal(ks[3], (E, F, H), dtype=jnp.float32) * sc, 'b2': jnp.zeros((E, H), dtype=jnp.float32), 'gamma': jnp.ones((H,), dtype=jnp.float32), 'beta': jnp.zeros((H,), dtype=jnp.float32)}
    _L0_ffn_all = _L0_ffn_setup()
    _L0_ffn_in = {k: v for k, v in _L0_ffn_all.items() if k in ('gate_w', 'gate_b', 'w1', 'b1', 'w2', 'b2', 'gamma', 'beta')}
    del _L0_ffn_all
    return {'x': x, 'adj': adj, 'nodemask': nodemask, 'L0_gnn_W': _L0_gnn_in['W'], 'L0_gnn_b': _L0_gnn_in['b'], 'L0_gnn_a1': _L0_gnn_in['a1'], 'L0_gnn_a2': _L0_gnn_in['a2'], 'L0_gnn_att_b': _L0_gnn_in['att_b'], 'L0_ffn_gate_w': _L0_ffn_in['gate_w'], 'L0_ffn_gate_b': _L0_ffn_in['gate_b'], 'L0_ffn_w1': _L0_ffn_in['w1'], 'L0_ffn_b1': _L0_ffn_in['b1'], 'L0_ffn_w2': _L0_ffn_in['w2'], 'L0_ffn_b2': _L0_ffn_in['b2'], 'L0_ffn_gamma': _L0_ffn_in['gamma'], 'L0_ffn_beta': _L0_ffn_in['beta']}

def reference(x, adj, nodemask, L0_gnn_W, L0_gnn_b, L0_gnn_a1, L0_gnn_a2, L0_gnn_att_b, L0_ffn_gate_w, L0_ffn_gate_b, L0_ffn_w1, L0_ffn_b1, L0_ffn_w2, L0_ffn_b2, L0_ffn_gamma, L0_ffn_beta):
    import jax
    import jax.numpy as jnp

    def _L0_gnn_ref(x, adj, mask, W, b, a1, a2, att_b):
        import jax, jax.numpy as jnp
        import numpy as np
        B, N, IN_DIM, OUT_DIM = (8, 1024, 128, 128)
        EDGE_P = 0.02
        MASK_P = 0.9
        h = jnp.einsum('bni,di->bnd', x, W) + b
        s1 = h @ a1
        s2 = h @ a2
        logits = s1[:, :, None] + s2[:, None, :] + att_b
        att = jax.nn.sigmoid(logits) * adj
        att = att * mask[:, :, None] * mask[:, None, :]
        att = att / (jnp.sum(att, axis=-1, keepdims=True) + 1e-08)
        h_new = jnp.einsum('bij,bjd->bid', att, h)
        return h_new * mask[:, :, None]

    def _L0_ffn_ref(x, gate_w, gate_b, w1, b1, w2, b2, gamma, beta):
        import jax, jax.numpy as jnp
        import numpy as np
        B, S, H, F, E, K = (8, 2048, 128, 256, 16, 2)
        EPS = 1e-05
        gate_logits = x @ gate_w + gate_b
        topk_vals, topk_idx = jax.lax.top_k(gate_logits, K)
        topk_w = jax.nn.softmax(topk_vals, axis=-1)
        h = jax.nn.relu(jnp.einsum('bsh,ehf->bsef', x, w1) + b1)
        expert_out = jnp.einsum('bsef,efh->bseh', h, w2) + b2
        sel = jnp.take_along_axis(expert_out, topk_idx[:, :, :, None], axis=2)
        moe = jnp.sum(topk_w[..., None] * sel, axis=2)
        y = x + moe
        mu = jnp.mean(y, axis=-1, keepdims=True)
        var = jnp.var(y, axis=-1, keepdims=True)
        return (y - mu) / jnp.sqrt(var + EPS) * gamma + beta
    x = x + _L0_gnn_ref(_layernorm(x, axis=-1), adj, nodemask, L0_gnn_W, L0_gnn_b, L0_gnn_a1, L0_gnn_a2, L0_gnn_att_b)
    x = x + _L0_ffn_ref(_layernorm(x, axis=-1), L0_ffn_gate_w, L0_ffn_gate_b, L0_ffn_w1, L0_ffn_b1, L0_ffn_w2, L0_ffn_b2, L0_ffn_gamma, L0_ffn_beta)
    return x

_drawn_inputs = setup_inputs


def setup_inputs(seed=0):
    import zlib

    import numpy as np

    out = dict(_drawn_inputs(seed))
    spreads = {'L0_ffn_gate_b': (0.0, 0.1),
     'L0_ffn_b1': (0.0, 0.8),
     'L0_ffn_b2': (0.0, 0.1),
     'L0_ffn_gamma': (1.0, 0.2),
     'L0_ffn_beta': (0.0, 0.1)}
    factors = {'L0_gnn_a1': 8.0, 'L0_ffn_w1': 3.647, 'L0_ffn_w2': 2.863}
    for name, (base, spread) in spreads.items():
        noise = np.random.default_rng([zlib.crc32(name.encode()), seed]).standard_normal(out[name].shape)
        drawn = base * np.exp(spread * noise) if base else spread * noise
        out[name] = jnp.asarray(drawn.astype(out[name].dtype))
    for name, factor in factors.items():
        out[name] = (out[name] * factor).astype(out[name].dtype)
    return out
```

```python
from contextlib import ExitStack

import concourse.bass as bass
from concourse import mybir

F32 = mybir.dt.float32
BF16 = mybir.dt.bfloat16
I32 = mybir.dt.int32
U32 = mybir.dt.uint32
ALU = mybir.AluOpType
ACT = mybir.ActivationFunctionType
AX = mybir.AxisListType.X

P = 128
D = 128
GRAPHS, NODES = 32, 256
TPG = NODES // P
PAIRS = GRAPHS // 2
TPP = 2 * TPG
TILES = GRAPHS * TPG
TOKENS = GRAPHS * NODES
XCHUNKS = 4
TPX = TILES // XCHUNKS
EXPERTS, HID, TOPK = 16, 256, 2
FC = HID // P
BT = 256
TPB = BT // P
RING = 4
NBLK = -(-(TOKENS * TOPK // BT + EXPERTS) // RING) * RING
BTURNS = NBLK // RING
CAP = TOKENS + BT
PAD_ROW = EXPERTS * CAP
RW = D + 2
B1, B2, ENO = HID + FC * D, HID + FC * D + FC, HID + FC * D + FC + D
WCOLS = ENO + 1
HA = D + 2
GT = 4
GROUPS = TILES // GT
SCATTERS = TPP * TOPK
EPS = 1e-5


def begun(turn):
    return not isinstance(turn, int) or turn > 0


def build(nc, x, adj, nodemask, gnn_w, gnn_b, gnn_a1, gnn_a2, att_b, gate_w, gate_b, experts, gamma, beta, out):
    ctx = ExitStack()
    with ctx:
        def sb(name, shape, dt=F32):
            return ctx.enter_context(nc.sbuf_tensor(name, shape, dt))

        def sem(name):
            return ctx.enter_context(nc.semaphore(name))

        sorted_x = nc.dram_tensor("sorted_x", (PAD_ROW + BT, RW), F32, kind="Internal").ap()
        token_y = nc.dram_tensor("token_y", (TOKENS * TOPK, D), F32, kind="Internal").ap()

        ident = sb("ident", [P, P])
        before = sb("before", [P, P], BF16)
        ones = sb("ones", [P, P], BF16)
        ones_f = sb("ones_f", [P, P])
        pad_rows = sb("pad_rows", [P, TPB, RW])
        token2 = sb("token2", [P, TILES])
        iota_e = sb("iota_e", [P, EXPERTS])
        iota_p = sb("iota_p", [P, 1])
        first_row = sb("first_row", [P, EXPERTS])
        neg_half = sb("neg_half", [P, TPX])
        eps_t = sb("eps_t", [P, 1])
        w_raw = sb("w_raw", [D, D])
        mask_rows = sb("mask_rows", [TILES, P])
        vec = sb("vec", [P, 4])
        a1_bc = sb("a1_bc", [P, P])
        w_aug = sb("w_aug", [P, HA])
        u1_bc = sb("u1_bc", [P, P])
        h_bias = sb("h_bias", [1, HA])
        att_b_sb = sb("att_b_sb", [1, 1])
        gate_w_sb = sb("gate_w_sb", [D, EXPERTS])
        gate_b_bc = sb("gate_b_bc", [P, EXPERTS])
        gamma_bc = sb("gamma_bc", [P, D])
        beta_bc = sb("beta_bc", [P, D])
        mask_t = sb("mask_t", [P, TILES])
        mask_sq = sb("mask_sq", [P, TILES])

        xmid = sb("xmid", [P, TILES, D])
        xn2_all = sb("xn2_all", [P, TILES, D])
        mv1 = sb("mv1", [P, TILES, 2])
        rs1 = sb("rs1", [P, TILES])
        rstd1 = sb("rstd1", [P, TILES])
        lead = sb("lead", [P, TILES])
        weight = sb("weight", [P, TILES, TOPK])

        adj_in = sb("adj_in", [P, 2, TPG, NODES])
        st1 = sb("st1", [P, TPX, 6])
        xn = sb("xn", [P, TPP, D])
        xnT = sb("xnT", [P, TPP * P])
        h_sb = sb("h_sb", [P, 2, TPG, HA])
        sig = sb("sig", [P, 2, TPG, NODES])
        att = sb("att", [P, 2, TPG, NODES])
        den = sb("den", [P, 4, 2, TPG])
        st2 = sb("st2", [P, TPP, 6])
        mv2 = sb("mv2", [P, TPP, 2])
        rs2 = sb("rs2", [P, 2, TPP])
        xn2 = sb("xn2", [P, 2, TPP, RW])
        xn2T = sb("xn2T", [P, TPP * P])
        logits = sb("logits", [P, TPP, EXPERTS])
        m8 = sb("m8", [P, TPP, 8])
        i8 = sb("i8", [P, TPP, 8], U32)
        onehot = sb("onehot", [P, TPP, TOPK, EXPERTS])
        chosen = sb("chosen", [P, TPP, EXPERTS], BF16)
        count = sb("count", [P, EXPERTS])
        row_of = sb("row_of", [P, TPP, EXPERTS])
        picked = sb("picked", [P, TPP, TOPK, EXPERTS])
        rows = sb("rows", [P, 2, TPP, TOPK], I32)

        cnt_i = sb("cnt_i", [P, 2, EXPERTS], I32)
        nblk = sb("nblk", [P, EXPERTS])
        last_blk = sb("last_blk", [P, EXPERTS])
        past = sb("past", [P, 2, EXPERTS])
        blk = sb("blk", [P, 8])
        tab = sb("tab", [1, 2 * P], I32)
        fill_row = sb("fill_row", [P, EXPERTS], I32)

        xb = sb("xb", [P, RING, TPB, RW])
        wb = sb("wb", [P, RING, WCOLS])
        xbT = sb("xbT", [P, RING, BT])
        hid = sb("hid", [P, RING, FC, BT])
        yb = sb("yb", [P, RING, TPB, D])
        y_row = sb("y_row", [P, RING, TPB], I32)

        got = sb("got", [P, 2, GT, TOPK, D])
        y = sb("y", [P, 2, GT, D])
        st3 = sb("st3", [P, 2, GT, 6])
        mv3 = sb("mv3", [P, 2, GT, 2])
        rs3 = sb("rs3", [P, 2, 3, GT])
        z = sb("z", [P, 2, GT, D])
        zg = sb("zg", [P, 2, GT, D])
        res = sb("res", [P, 2, GT, D])

        psum = ctx.enter_context(nc.psum_tensor("psum", [P, 8, 512], F32))
        xT_ps, adjT_ps, h_ps, s1_ps, agg_ps, route_ps = (
            psum[:, 0, :], psum[:, 1:3, :], psum[:, 3, :], psum[:, 4, :], psum[:, 5:7, :], psum[:, 7, :])
        agg_v = agg_ps[:, :, 0:TPG * (D + 1)].rearrange("p g (t c) -> p g t c", c=D + 1)
        h_v = h_ps[:, 0:TPG * HA].rearrange("p (t c) -> p t c", c=HA)
        gate_v = route_ps[:, 0:TPP * EXPERTS].rearrange("p (t e) -> p t e", e=EXPERTS)
        rank_v = route_ps[:, TPP * EXPERTS:2 * TPP * EXPERTS].rearrange("p (t e) -> p t e", e=EXPERTS)
        total_v = route_ps[:, 2 * TPP * EXPERTS:(2 * TPP + 1) * EXPERTS]

        weights_in, consts_in, late_in = sem("weights_in"), sem("consts_in"), sem("late_in")
        const_done = sem("const_done")
        pool_step, dve_step = sem("pool_step"), sem("dve_step")
        setup_pe, setup_dve = sem("setup_pe"), sem("setup_dve")
        x_in = [sem(f"x_in{c}") for c in range(XCHUNKS)]
        adj_in_s = [sem(f"adj_in{p}") for p in range(2)]
        stats1, rstd1_done, xn_done = sem("stats1"), sem("rstd1_done"), sem("xn_done")
        xT_done, xT_copied = sem("xT_done"), sem("xT_copied")
        adjT_g, h_g, s1_done, h_sb_g, sig_g, att_g = (
            sem("adjT_g"), sem("h_g"), sem("s1_done"), sem("h_sb_g"), sem("sig_g"), sem("att_g"))
        agg_g, xmid_done = sem("agg_g"), sem("xmid_done")
        stats2, rstd2_done, xn2_done, xn2_kept = sem("stats2"), sem("rstd2_done"), sem("xn2_done"), sem("xn2_kept")
        x2T_done, x2T_copied, gate_done = sem("x2T_done"), sem("x2T_copied"), sem("gate_done")
        chosen_done, rank_done, rows_done = sem("chosen_done"), sem("rank_done"), sem("rows_done")
        scattered = [sem(f"scattered{p}") for p in range(2)]
        fill_done, table_cols, table_ps, table_done, filled = (
            sem("fill_done"), sem("table_cols"), sem("table_ps"), sem("table_done"), sem("filled"))
        weight_done = sem("weight_done")
        block_in = [sem(f"block_in{q}") for q in range(RING)]
        xbT_ps_done, xbT_done, l1_done, hid_done, l2_done, yb_done = (
            sem("xbT_ps_done"), sem("xbT_done"), sem("l1_done"), sem("hid_done"), sem("l2_done"), sem("yb_done"))
        yb_out = [sem(f"yb_out{q}") for q in range(RING)]
        got_in = [sem(f"got_in{h}") for h in range(2)]
        y_done, std_done, shift_done, z_done, res_done = (
            sem("y_done"), sem("std_done"), sem("shift_done"), sem("z_done"), sem("res_done"))
        res_out = [sem(f"res_out{h}") for h in range(2)]
        pool_passed, dve_passed = sem("pool_passed"), sem("dve_passed")

        x_v = x.rearrange("g (t p) c -> p (g t) c", p=P)
        out_v = out.rearrange("g (t p) c -> p (g t) c", p=P)
        adj_v = adj.rearrange("g (t p) n -> g p t n", p=P)
        token_v = token_y.rearrange("(t p k) c -> p t k c", p=P, k=TOPK)
        block = ctx.enter_context(nc.Block())

        @block.sync
        def _(sp):
            for dst, src in ((w_raw[:, :], gnn_w), (vec[:, 0:1], gnn_a1.rearrange("(p a) -> p a", a=1)),
                             (vec[:, 1:2], gnn_a2.rearrange("(p a) -> p a", a=1)),
                             (vec[:, 2:3], gnn_b.rearrange("(p a) -> p a", a=1)),
                             (h_bias[:, 0:D], gnn_b.rearrange("(a c) -> a c", a=1)),
                             (att_b_sb[:, :], att_b.rearrange("(a c) -> a c", a=1))):
                sp.dma_start(dst, src).then_inc(weights_in, 16)
            sp.dma_start(mask_rows[:, :], nodemask.rearrange("g (t p) -> (g t) p", p=P)).then_inc(consts_in, 16)

            def load_adj(i):
                for p in range(2):
                    if begun(i):
                        sp.wait_ge(adjT_g, 2 * i + p - 1)
                    sp.dma_start(adj_in[:, p, :, :], adj_v[2 * i + p, :, :, :]).then_inc(adj_in_s[p], 16)

            load_adj(0)
            for dst, src in ((gate_w_sb[:, :], gate_w), (gate_b_bc[:, :], gate_b.partition_broadcast(P)),
                             (gamma_bc[:, :], gamma.partition_broadcast(P)),
                             (beta_bc[:, :], beta.partition_broadcast(P))):
                sp.dma_start(dst, src).then_inc(late_in, 16)
            with sp.Fori(1, PAIRS) as i:
                load_adj(i)

            sp.dma_start(sorted_x[PAD_ROW:PAD_ROW + BT, :].rearrange("(p t) c -> p t c", t=TPB),
                         pad_rows[:, :, :]).then_inc(filled, 16)
            sp.wait_ge(fill_done, 1)
            for e in range(0, EXPERTS, 2):
                row = sp.value_load(fill_row[0:1, e:e + 1], min_val=0, max_val=PAD_ROW - BT)
                sp.dma_start(sorted_x[bass.ds(row, BT), :].rearrange("(p t) c -> p t c", t=TPB),
                             pad_rows[:, :, :]).then_inc(filled, 16)
            sp.wait_ge(table_done, 1)

            def load_block(k, q):
                b = k * RING + q
                e = sp.value_load(tab[0:1, bass.ds(b, 1)], min_val=0, max_val=EXPERTS - 1)
                row = sp.value_load(tab[0:1, bass.ds(b + P, 1)], min_val=0, max_val=PAD_ROW)
                if begun(k):
                    sp.wait_ge(yb_done, b - RING + 1)
                sp.dma_start(wb[:, q, :], experts[bass.ds(e, 1), :, :].rearrange("a p c -> p (a c)")
                             ).then_inc(block_in[q], 16)
                if not begun(k) and q == 0:
                    sp.wait_ge(filled, 16 * (EXPERTS + 1))
                    sp.wait_ge(scattered[0], 16 * SCATTERS * PAIRS // 2)
                    sp.wait_ge(scattered[1], 16 * SCATTERS * PAIRS // 2)
                sp.dma_start(xb[:, q, :, :], sorted_x[bass.ds(row, BT), :].rearrange("(p t) c -> p t c", t=TPB)
                             ).then_inc(block_in[q], 16)

            for q in range(RING):
                load_block(0, q)
            with sp.Fori(1, BTURNS) as k:
                for q in range(RING):
                    load_block(k, q)

            for q in range(RING):
                sp.wait_ge(yb_out[q], 16 * TPB * BTURNS)

            def load_group(k, h):
                g = 2 * k + h
                if begun(k):
                    sp.wait_ge(y_done, g - 1)
                sp.dma_start(got[:, h, :, :, :], token_v[:, bass.ds(g * GT, GT), :, :]).then_inc(got_in[h], 16)

            def store_group(k, h):
                g = 2 * k + h
                sp.wait_ge(res_done, g + 1)
                sp.dma_start(out_v[:, bass.ds(g * GT, GT), :], res[:, h, :, :]).then_inc(res_out[h], 16)

            load_group(0, 0)
            load_group(0, 1)
            with sp.Fori(1, GROUPS // 2) as k:
                for h in range(2):
                    load_group(k, h)
                    store_group(k - 1, h)
            for h in range(2):
                store_group(GROUPS // 2 - 1, h)
            for h in range(2):
                sp.wait_ge(res_out[h], 16 * (GROUPS // 2))

        @block.gpsimd
        def _(pool):
            g = nc.gpsimd
            g.memset(ident[:, :], 0.0).then_inc(pool_step, 1)
            g.memset(before[:, :], 1.0).then_inc(pool_step, 1)
            g.memset(pad_rows[:, :, :], 0.0).then_inc(pool_step, 1)
            g.memset(ones[:, :], 1.0).then_inc(const_done, 1)
            g.memset(ones_f[:, :], 1.0).then_inc(const_done, 1)
            g.memset(neg_half[:, :], -0.5).then_inc(const_done, 1)
            g.memset(eps_t[:, :], EPS).then_inc(const_done, 1)
            pool.wait_ge(pool_step, 3)
            g.affine_select(out=ident[:, :], in_=ident[:, :], compare_op=ALU.not_equal, fill=1.0, base=0,
                            pattern=[[-1, P]], channel_multiplier=1).then_inc(const_done, 1)
            g.affine_select(out=before[:, :], in_=before[:, :], compare_op=ALU.is_gt, fill=0.0, base=0,
                            pattern=[[1, P]], channel_multiplier=-1).then_inc(const_done, 1)
            for dst, pattern, base, by_partition in (
                    (iota_e[:, :], [[1, EXPERTS]], 0, 0), (iota_p[:, :], [[0, 1]], 0, 1),
                    (first_row[:, :], [[CAP, EXPERTS]], 0, 0), (token2[:, :], [[2 * P, TILES]], 0, 2),
                    (pad_rows[:, :, D], [[2, TPB]], 2 * TOKENS, 2 * TPB)):
                g.iota(dst, pattern=pattern, base=base, channel_multiplier=by_partition,
                       allow_small_or_imprecise_dtypes=True).then_inc(const_done, 1)

            for c in range(XCHUNKS):
                s = slice(c * TPX, (c + 1) * TPX)
                pool.wait_ge(stats1, c + 1)
                g.tensor_scalar(rs1[:, s], mv1[:, s, 1], EPS, None, ALU.add).then_inc(pool_step, 1)
                pool.wait_ge(pool_step, 4 + c)
                g.tensor_tensor(rstd1[:, s], rs1[:, s], neg_half[:, :], ALU.pow).then_inc(rstd1_done, 1)
            first_step = 3 + XCHUNKS

            def rstd2(i):
                pool.wait_ge(stats2, i + 1)
                pool.sem_inc(pool_passed, 1)
                g.tensor_scalar(rs2[:, 0, :], mv2[:, :, 1], EPS, None, ALU.add).then_inc(pool_step, 1)
                pool.wait_ge(pool_step, first_step + i + 1)
                g.tensor_tensor(rs2[:, 1, :], rs2[:, 0, :], neg_half[:, 0:TPP], ALU.pow).then_inc(rstd2_done, 1)

            def scatter(i, slot):
                pool.wait_ge(xn2_kept, i + 1)
                pool.wait_ge(rows_done, i + 1)
                pool.sem_inc(pool_passed, 1)
                for t in range(TPP):
                    for k in range(TOPK):
                        pool.indirect_dma_start(
                            sorted_x, bass.IndirectOffsetOnAxis(ap=rows[:, slot, t, k:k + 1], axis=0),
                            xn2[:, slot, t, :], None).then_inc(scattered[slot], 16)

            rstd2(0)
            with pool.Fori(0, (PAIRS - 2) // 2) as j:
                for s in range(2):
                    rstd2(2 * j + s + 1)
                    scatter(2 * j + s, s)
            rstd2(PAIRS - 1)
            scatter(PAIRS - 2, 0)
            scatter(PAIRS - 1, 1)

            with pool.Fori(0, BTURNS) as k:
                for q in range(RING):
                    pool.wait_ge(yb_done, k * RING + q + 1)
                    pool.sem_inc(pool_passed, 1)
                    for t in range(TPB):
                        pool.indirect_dma_start(
                            token_y, bass.IndirectOffsetOnAxis(ap=y_row[:, q, t:t + 1], axis=0), yb[:, q, t, :], None,
                            bounds_check=TOKENS * TOPK - 1, oob_is_err=False).then_inc(yb_out[q], 16)

        @block.scalar
        def _(act):
            for c in range(XCHUNKS):
                s = slice(c * TPX, (c + 1) * TPX)
                act.dma_start(xmid[:, s, :], x_v[:, s, :]).then_inc(x_in[c], 16)

            def front(i):
                act.wait_ge(xT_done, i + 1)
                if begun(i):
                    act.wait_ge(h_g, 2 * i)
                act.copy(xnT[:, :], xT_ps).then_inc(xT_copied, 1)
                for p in range(2):
                    act.wait_ge(h_g, 2 * i + p + 1)
                    if begun(i):
                        act.wait_ge(agg_g, 2 * i + p - 1)
                    act.copy(h_sb[:, p, :, :], h_v).then_inc(h_sb_g, 1)
                act.wait_ge(s1_done, i + 1)
                for p in range(2):
                    act.wait_ge(h_sb_g, 2 * i + p + 1)
                    if begun(i):
                        act.wait_ge(att_g, 2 * i + p - 1)
                    for t in range(TPG):
                        last = act.activation(sig[:, p, t, :], s1_ps[:, p * NODES:(p + 1) * NODES], ACT.Sigmoid,
                                              bias=h_sb[:, p, t, HA - 1:HA])
                    last.then_inc(sig_g, 1)

            def middle(i, slot):
                act.wait_ge(x2T_done, i + 1)
                if begun(i):
                    act.wait_ge(gate_done, i)
                act.copy(xn2T[:, :], xT_ps).then_inc(x2T_copied, 1)
                act.copy(xn2[:, slot, :, D], token2[:, bass.ds(i * TPP, TPP)]).then_inc(xn2_kept, 1)
                act.copy(xn2_all[:, bass.ds(i * TPP, TPP), :], xn2[:, slot, :, 0:D])

            act.wait_ge(const_done, 11)
            front(0)
            front(1)
            middle(0, 0)
            with act.Fori(0, (PAIRS - 2) // 2) as j:
                for s in range(2):
                    front(2 * j + s + 2)
                    middle(2 * j + s + 1, 1 - s)
            middle(PAIRS - 1, 1)

            act.wait_ge(fill_done, 1)
            for e in range(1, EXPERTS, 2):
                row = act.value_load(fill_row[0:1, e:e + 1], min_val=0, max_val=PAD_ROW - BT)
                act.dma_start(sorted_x[bass.ds(row, BT), :].rearrange("(p t) c -> p t c", t=TPB),
                              pad_rows[:, :, :]).then_inc(filled, 16)
            for n in range(TOPK):
                act.activation(weight[:, :, n], lead[:, :], ACT.Sigmoid, scale=1.0 - 2.0 * n).then_inc(weight_done, 1)

            def relu(k, q):
                b = k * RING + q
                act.wait_ge(l1_done, b + 1)
                if begun(k):
                    act.wait_ge(l2_done, b - RING + 1)
                for c in range(FC):
                    last = act.activation(hid[:, q, c, :], psum[:, 2 + q % 2, c * BT:(c + 1) * BT], ACT.Relu,
                                          bias=wb[:, q, B1 + c:B1 + c + 1])
                last.then_inc(hid_done, 1)

            for q in range(RING):
                relu(0, q)
            with act.Fori(1, BTURNS) as k:
                for q in range(RING):
                    relu(k, q)

            def deviation(k, h):
                act.wait_ge(y_done, 2 * k + h + 1)
                act.activation(rs3[:, h, 0, :], mv3[:, h, :, 1], ACT.Sqrt, bias=eps_t[:, :]).then_inc(std_done, 1)

            def normalise(k, h):
                g = 2 * k + h
                act.wait_ge(shift_done, g + 1)
                if begun(k):
                    act.wait_ge(res_done, g - 1)
                for t in range(GT):
                    last = act.activation(z[:, h, t, :], y[:, h, t, :], ACT.Identity, bias=rs3[:, h, 2, t:t + 1],
                                          scale=rs3[:, h, 1, t:t + 1])
                last.then_inc(z_done, 1)

            for h in range(2):
                deviation(0, h)
                normalise(0, h)
            with act.Fori(1, GROUPS // 2) as k:
                for h in range(2):
                    deviation(k, h)
                    normalise(k, h)

        @block.vector
        def _(dve):
            v = nc.vector
            steps = [0]

            def step(instruction):
                instruction.then_inc(dve_step, 1)
                steps[0] = steps[0] + 1
                return steps[0]

            dve.wait_ge(weights_in, 16 * 6)
            v.tensor_copy(a1_bc[:, :], vec[:, 0:1].broadcast_to([P, P])).then_inc(setup_dve, 1)
            v.tensor_tensor(vec[:, 3:4], vec[:, 0:1], vec[:, 1:2], ALU.add).then_inc(setup_dve, 1)
            v.memset(h_bias[:, D:D + 1], 1.0).then_inc(setup_dve, 1)
            v.memset(w_aug[:, D:D + 1], 0.0).then_inc(setup_dve, 1)
            dve.wait_ge(const_done, 11)
            step(v.tensor_copy(count[:, :], first_row[:, :]))
            dve.wait_ge(setup_pe, 1)
            v.tensor_copy(w_aug[:, 0:D], psum[:, 0, 0:P]).then_inc(setup_dve, 1)
            v.tensor_copy(w_aug[:, D + 1:D + 2], psum[:, 0, P:P + 1]).then_inc(setup_dve, 1)
            v.tensor_copy(u1_bc[:, :], psum[:, 0, 2 * P:3 * P]).then_inc(setup_dve, 1)
            v.tensor_tensor(h_bias[:, D + 1:D + 2], psum[0:1, 0, P + 1:P + 2], att_b_sb[:, :], ALU.add
                            ).then_inc(setup_dve, 1)
            n = step(v.tensor_copy(mask_t[:, :], psum[:, 1, 0:TILES]))
            dve.wait_ge(dve_step, n)
            step(v.tensor_tensor(mask_sq[:, :], mask_t[:, :], mask_t[:, :], ALU.mult))

            for c in range(XCHUNKS):
                dve.wait_ge(x_in[c], 16)
                if c:
                    dve.wait_ge(stats1, c)
                for t in range(TPX):
                    n = step(v.bn_stats(st1[:, t, :], xmid[:, c * TPX + t, :]))
                dve.wait_ge(dve_step, n)
                for t in range(TPX):
                    last = v.bn_aggr(mv1[:, c * TPX + t, :], st1[:, t, :])
                last.then_inc(stats1, 1)
            dve.wait_ge(rstd1_done, XCHUNKS)

            def norm1(i):
                if begun(i):
                    dve.wait_ge(xT_done, i)
                for t in range(TPP):
                    last = v.tensor_scalar(xn[:, t, :], xmid[:, bass.ds(i * TPP + t, 1), :].rearrange("p a c -> p (a c)"),
                                           mv1[:, bass.ds(i * TPP + t, 1), 0], rstd1[:, bass.ds(i * TPP + t, 1)],
                                           ALU.subtract, ALU.mult)
                last.then_inc(xn_done, 1)

            def attention(i):
                for p in range(2):
                    dve.wait_ge(adjT_g, 2 * i + p + 1)
                    dve.wait_ge(sig_g, 2 * i + p + 1)
                    if begun(i):
                        dve.wait_ge(agg_g, 2 * i + p - 1)
                    for t in range(TPG):
                        last = v.scalar_tensor_tensor(
                            out=att[:, p, t, :], in0=adjT_ps[:, p, t * NODES:(t + 1) * NODES],
                            scalar=mask_t[:, bass.ds((2 * i + p) * TPG + t, 1)], in1=sig[:, p, t, :],
                            op0=ALU.mult, op1=ALU.mult)
                    last.then_inc(att_g, 1)

            def residual(i):
                tiles = bass.ds(i * TPP, TPP)
                dve.wait_ge(agg_g, 2 * i + 2)
                n = step(v.tensor_tensor(den[:, 0, :, :], agg_v[:, :, :, D],
                                         mask_t[:, tiles].rearrange("p (g t) -> p g t", t=TPG), ALU.mult))
                dve.wait_ge(dve_step, n)
                n = step(v.tensor_scalar(den[:, 1, :, :], den[:, 0, :, :], 1e-8, None, ALU.add))
                dve.wait_ge(dve_step, n)
                n = step(v.reciprocal(den[:, 2, :, :], den[:, 1, :, :]))
                dve.wait_ge(dve_step, n)
                n = step(v.tensor_tensor(den[:, 3, :, :], den[:, 2, :, :],
                                         mask_sq[:, tiles].rearrange("p (g t) -> p g t", t=TPG), ALU.mult))
                dve.wait_ge(dve_step, n)
                for t in range(TPP):
                    row = xmid[:, bass.ds(i * TPP + t, 1), :].rearrange("p a c -> p (a c)")
                    ins = v.scalar_tensor_tensor(out=row, in0=agg_v[:, t // TPG, t % TPG, 0:D],
                                                 scalar=den[:, 3, t // TPG, t % TPG:t % TPG + 1],
                                                 in1=row, op0=ALU.mult, op1=ALU.add)
                ins.then_inc(xmid_done, 1)
                dve.wait_ge(xmid_done, i + 1)
                dve.sem_inc(dve_passed, 1)
                for t in range(TPP):
                    n = step(v.bn_stats(st2[:, t, :], xmid[:, bass.ds(i * TPP + t, 1), :].rearrange("p a c -> p (a c)")))
                dve.wait_ge(dve_step, n)
                dve.sem_inc(dve_passed, 1)
                for t in range(TPP):
                    last = v.bn_aggr(mv2[:, t, :], st2[:, t, :])
                last.then_inc(stats2, 1)

            def norm2(i, slot, before_it):
                dve.wait_ge(rstd2_done, i + 1)
                if before_it is not None:
                    dve.wait_ge(scattered[slot], 16 * SCATTERS * before_it)
                    dve.wait_ge(x2T_copied, i)
                for t in range(TPP):
                    last = v.tensor_scalar(xn2[:, slot, t, 0:D],
                                           xmid[:, bass.ds(i * TPP + t, 1), :].rearrange("p a c -> p (a c)"),
                                           mv2[:, t, 0:1], rs2[:, 1, t:t + 1], ALU.subtract, ALU.mult)
                last.then_inc(xn2_done, 1)

            def route(i, slot):
                dve.wait_ge(gate_done, i + 1)
                n = step(v.tensor_tensor(logits[:, :, :], gate_v, gate_b_bc[:, None, :].broadcast_to([P, TPP, EXPERTS]),
                                         ALU.add))
                dve.wait_ge(dve_step, n)
                dve.sem_inc(dve_passed, 1)
                for t in range(TPP):
                    n = step(v.max(m8[:, t, :], logits[:, t, :]))
                dve.wait_ge(dve_step, n)
                dve.sem_inc(dve_passed, 1)
                for t in range(TPP):
                    n = step(v.max_index(i8[:, t, :], m8[:, t, :], logits[:, t, :]))
                v.tensor_tensor(lead[:, bass.ds(i * TPP, TPP)], m8[:, :, 0], m8[:, :, 1], ALU.subtract)
                dve.wait_ge(dve_step, n)
                n = step(v.tensor_tensor(onehot[:, :, :, :],
                                         i8[:, :, 0:TOPK].rearrange("p t (k a) -> p t k a", a=1).broadcast_to([P, TPP, TOPK, EXPERTS]),
                                         iota_e[:, None, None, :].broadcast_to([P, TPP, TOPK, EXPERTS]), ALU.is_equal))
                v.tensor_copy(xn2[:, slot, :, D + 1], i8[:, :, 0])
                dve.wait_ge(dve_step, n)
                v.tensor_tensor(chosen[:, :, :], onehot[:, :, 0, :], onehot[:, :, 1, :], ALU.add).then_inc(chosen_done, 1)

            def place(i, slot):
                dve.wait_ge(rank_done, i + 1)
                n = step(v.tensor_tensor(row_of[:, :, :], rank_v, count[:, None, :].broadcast_to([P, TPP, EXPERTS]), ALU.add))
                dve.wait_ge(dve_step, n)
                step(v.tensor_tensor(count[:, :], count[:, :], total_v, ALU.add))
                n = step(v.tensor_tensor(picked[:, :, :, :], onehot[:, :, :, :],
                                         row_of[:, :, None, :].broadcast_to([P, TPP, TOPK, EXPERTS]), ALU.mult))
                dve.wait_ge(dve_step, n)
                with nc.allow_low_precision(reason="whole numbers below 2**24 are summed in float32, then stored as int32"):
                    v.tensor_reduce(rows[:, slot, :, :], picked[:, :, :, :], axis=AX, op=ALU.add).then_inc(rows_done, 1)

            def turn(m, slot, before_it):
                norm1(m)
                residual(m - 1)
                route(m - 2, slot)
                attention(m)
                place(m - 2, slot)
                norm2(m - 1, 1 - slot, before_it)

            norm1(0)
            attention(0)
            norm1(1)
            residual(0)
            attention(1)
            norm2(0, 0, None)
            turn(2, 0, None)
            base = steps[0]
            turn(3, 1, 1)
            per = steps[0] - base
            with dve.Fori(0, (PAIRS - 4) // 2) as j:
                for s in range(2):
                    steps[0] = base + per + j * (2 * per) + s * per
                    turn(2 * j + 4 + s, s, j + 1 + s)
            steps[0] = base + per * (PAIRS - 3)
            residual(PAIRS - 1)
            route(PAIRS - 2, 0)
            place(PAIRS - 2, 0)
            norm2(PAIRS - 1, 1, PAIRS // 2 - 1)
            route(PAIRS - 1, 1)
            place(PAIRS - 1, 1)

            dve.wait_ge(dve_step, steps[0])
            v.tensor_copy(fill_row[:, :], count[:, :]).then_inc(fill_done, 1)
            n = step(v.scalar_tensor_tensor(out=past[:, 0, :], in0=count[:, :], scalar=float(BT - 1), in1=first_row[:, :],
                                            op0=ALU.add, op1=ALU.subtract))
            dve.wait_ge(dve_step, n)
            n = step(v.tensor_copy(cnt_i[:, 0, :], past[:, 0, :]))
            dve.wait_ge(dve_step, n)
            n = step(v.tensor_scalar(cnt_i[:, 1, :], cnt_i[:, 0, :], BT.bit_length() - 1, None, ALU.arith_shift_right))
            dve.wait_ge(dve_step, n)
            n = step(v.tensor_copy(nblk[:, :], cnt_i[:, 1, :]))
            dve.wait_ge(dve_step, n)
            n = step(v.tensor_tensor_scan(last_blk[:, :], ones_f[:, 0:EXPERTS], nblk[:, :], 0.0, ALU.mult, ALU.add))
            dve.wait_ge(dve_step, n)
            n = step(v.tensor_scalar(past[:, 0, :], last_blk[:, :], iota_p[:, :], None, ALU.is_le))
            dve.wait_ge(dve_step, n)
            step(v.tensor_reduce(blk[:, 0:1], past[:, 0, :], axis=AX, op=ALU.add))
            n = step(v.tensor_tensor(past[:, 1, :], past[:, 0, :], nblk[:, :], ALU.mult))
            dve.wait_ge(dve_step, n)
            n = step(v.tensor_reduce(blk[:, 1:2], past[:, 1, :], axis=AX, op=ALU.add))
            dve.wait_ge(dve_step, n)
            step(v.tensor_scalar(blk[:, 3:4], blk[:, 0:1], float(EXPERTS - 1), None, ALU.min))
            step(v.tensor_scalar(blk[:, 4:5], blk[:, 0:1], float(EXPERTS), None, ALU.is_lt))
            n = step(v.tensor_tensor(blk[:, 2:3], iota_p[:, :], blk[:, 1:2], ALU.subtract))
            dve.wait_ge(dve_step, n)
            n = step(v.scalar_tensor_tensor(out=blk[:, 5:6], in0=blk[:, 2:3], scalar=float(BT), in1=blk[:, 4:5],
                                            op0=ALU.mult, op1=ALU.mult))
            dve.wait_ge(dve_step, n)
            v.scalar_tensor_tensor(out=blk[:, 6:7], in0=blk[:, 0:1], scalar=float(CAP), in1=blk[:, 5:6],
                                   op0=ALU.mult, op1=ALU.add).then_inc(table_cols, 1)
            dve.wait_ge(table_ps, 1)
            v.tensor_copy(tab[:, :], psum[0:1, 0, 0:2 * P]).then_inc(table_done, 1)

            def block_x(k, q):
                b = k * RING + q
                dve.wait_ge(xbT_ps_done, b + 1)
                if begun(k):
                    dve.wait_ge(l1_done, b - RING + 1)
                    dve.wait_ge(yb_out[q], 16 * TPB * k)
                v.tensor_copy(xbT[:, q, :], psum[:, q % 2, 0:BT]).then_inc(xbT_done, 1)
                v.scalar_tensor_tensor(out=y_row[:, q, :], in0=xb[:, q, :, D + 1], scalar=wb[:, q, ENO:ENO + 1],
                                       in1=xb[:, q, :, D], op0=ALU.not_equal, op1=ALU.add)

            def block_y(b, q):
                dve.wait_ge(l2_done, b + 1)
                v.tensor_tensor(yb[:, q, :, :], psum[:, 4 + q % 2, 0:TPB * D].rearrange("p (t c) -> p t c", c=D),
                                wb[:, q, None, B2:B2 + D].broadcast_to([P, TPB, D]), ALU.add).then_inc(yb_done, 1)

            def add_beta(k):
                tiles = xmid[:, bass.ds(k * GT, GT), :]
                v.tensor_tensor(tiles, tiles, beta_bc[:, None, :].broadcast_to([P, GT, D]), ALU.add)

            for q in range(RING):
                block_x(0, q)
                if q >= 2:
                    block_y(q - 2, q - 2)
            with dve.Fori(1, 1 + GROUPS) as k:
                for q in range(RING):
                    block_x(k, q)
                    block_y(k * RING + q - 2, (q - 2) % RING)
                add_beta(k - 1)
            with dve.Fori(1 + GROUPS, BTURNS) as k:
                for q in range(RING):
                    block_x(k, q)
                    block_y(k * RING + q - 2, (q - 2) % RING)
            for b in (NBLK - 2, NBLK - 1):
                block_y(b, b % RING)

            dve.wait_ge(weight_done, TOPK)

            def combine(k, h):
                g = 2 * k + h
                dve.wait_ge(got_in[h], 16 * (k + 1))
                if begun(k):
                    dve.wait_ge(z_done, g - 1)
                for t in range(GT):
                    n = step(v.scalar_tensor_tensor(
                        out=y[:, h, t, :], in0=got[:, h, t, 0, :], scalar=weight[:, bass.ds(g * GT + t, 1), 0],
                        in1=xn2_all[:, bass.ds(g * GT + t, 1), :].rearrange("p a c -> p (a c)"),
                        op0=ALU.mult, op1=ALU.add))
                dve.wait_ge(dve_step, n)
                for t in range(GT):
                    n = step(v.scalar_tensor_tensor(
                        out=y[:, h, t, :], in0=got[:, h, t, 1, :], scalar=weight[:, bass.ds(g * GT + t, 1), 1],
                        in1=y[:, h, t, :], op0=ALU.mult, op1=ALU.add))
                dve.wait_ge(dve_step, n)
                dve.sem_inc(dve_passed, 1)
                for t in range(GT):
                    n = step(v.bn_stats(st3[:, h, t, :], y[:, h, t, :]))
                dve.wait_ge(dve_step, n)
                dve.sem_inc(dve_passed, 1)
                for t in range(GT):
                    last = v.bn_aggr(mv3[:, h, t, :], st3[:, h, t, :])
                last.then_inc(y_done, 1)

            def shift(g, h):
                dve.wait_ge(std_done, g + 1)
                n = step(v.reciprocal(rs3[:, h, 1, :], rs3[:, h, 0, :]))
                dve.wait_ge(dve_step, n)
                v.scalar_tensor_tensor(out=rs3[:, h, 2, :], in0=mv3[:, h, :, 0], scalar=-1.0, in1=rs3[:, h, 1, :],
                                       op0=ALU.mult, op1=ALU.mult).then_inc(shift_done, 1)

            def finish(k, h):
                g = 2 * k + h
                dve.wait_ge(z_done, g + 1)
                n = step(v.tensor_tensor(zg[:, h, :, :], z[:, h, :, :], gamma_bc[:, None, :].broadcast_to([P, GT, D]),
                                         ALU.mult))
                if begun(k):
                    dve.wait_ge(res_out[h], 16 * k)
                dve.wait_ge(dve_step, n)
                v.tensor_tensor(res[:, h, :, :], zg[:, h, :, :], xmid[:, bass.ds(g * GT, GT), :], ALU.add
                                ).then_inc(res_done, 1)

            combine(0, 0)
            shift(0, 0)
            combine(0, 1)
            finish(0, 0)
            shift(1, 1)
            base = steps[0]
            combine(1, 0)
            finish(0, 1)
            shift(2, 0)
            combine(1, 1)
            finish(1, 0)
            shift(3, 1)
            per = steps[0] - base
            with dve.Fori(2, GROUPS // 2) as k:
                steps[0] = base + (k - 1) * per
                combine(k, 0)
                finish(k - 1, 1)
                shift(2 * k, 0)
                combine(k, 1)
                finish(k, 0)
                shift(2 * k + 1, 1)
            steps[0] = base + (GROUPS // 2 - 1) * per
            finish(GROUPS // 2 - 1, 1)

        @block.tensor
        def _(pe):
            mm, tr = nc.tensor.matmul, nc.tensor.transpose

            pe.wait_ge(const_done, 11)
            pe.wait_ge(setup_dve, 4)
            tr(psum[:, 0, 0:P], w_raw[:, :], ident[:, :])
            mm(psum[:, 0, P:P + 1], w_raw[:, :], vec[:, 1:2], start=True, stop=True)
            mm(psum[0:1, 0, P + 1:P + 2], vec[:, 2:3], vec[:, 3:4], start=True, stop=True)
            mm(psum[:, 0, 2 * P:3 * P], w_raw[:, :], a1_bc[:, :], start=True, stop=True)
            pe.wait_ge(consts_in, 16)
            tr(psum[:, 1, 0:TILES], mask_rows[:, :], ident[0:TILES, 0:TILES]).then_inc(setup_pe, 1)
            pe.wait_ge(setup_dve, 8)
            pe.wait_ge(late_in, 16 * 4)

            def front(i):
                pe.wait_ge(xn_done, i + 1)
                if begun(i) and begun(i - 1 if isinstance(i, int) else i):
                    pe.wait_ge(x2T_copied, i - 1)
                for t in range(TPP):
                    last = tr(xT_ps[:, t * P:(t + 1) * P], xn[:, t, :], ident[:, :])
                last.then_inc(xT_done, 1)
                for p in range(2):
                    pe.wait_ge(adj_in_s[p], 16 * (i + 1))
                    if begun(i):
                        pe.wait_ge(att_g, 2 * i + p - 1)
                    for jt in range(TPG):
                        for it in range(TPG):
                            last = tr(adjT_ps[:, p, jt * NODES + it * P:jt * NODES + (it + 1) * P],
                                      adj_in[:, p, it, jt * P:(jt + 1) * P], ident[:, :])
                    last.then_inc(adjT_g, 1)
                pe.wait_ge(xT_copied, i + 1)
                for p in range(2):
                    if begun(i) or p:
                        pe.wait_ge(h_sb_g, 2 * i + p)
                    for t in range(TPG):
                        c = (p * TPG + t) * P
                        mm(h_v[:, t, :], xnT[:, c:c + P], w_aug[:, :], start=True, stop=False)
                        last = mm(h_v[:, t, :], ones_f[0:1, :], h_bias[:, :], start=False, stop=True)
                    if p == 0:
                        last.then_inc(h_g, 1)
                        if begun(i):
                            pe.wait_ge(sig_g, 2 * i)
                        mm(s1_ps, u1_bc[:, :], xnT[:, :], start=True, stop=True).then_inc(s1_done, 1)
                last.then_inc(h_g, 1)

            def aggregate(i):
                if begun(i):
                    pe.wait_ge(xmid_done, i)
                for p in range(2):
                    pe.wait_ge(h_sb_g, 2 * i + p + 1)
                    pe.wait_ge(att_g, 2 * i + p + 1)
                    for it in range(TPG):
                        for jt in range(TPG):
                            last = mm(agg_v[:, p, it, :], att[:, p, jt, it * P:(it + 1) * P], h_sb[:, p, jt, 0:D + 1],
                                      start=(jt == 0), stop=(jt == TPG - 1))
                    last.then_inc(agg_g, 1)

            def gate(i, slot, next_front):
                pe.wait_ge(xn2_done, i + 1)
                pe.wait_ge(xT_copied, next_front)
                for t in range(TPP):
                    last = tr(xT_ps[:, t * P:(t + 1) * P], xn2[:, slot, t, 0:D], ident[:, :])
                last.then_inc(x2T_done, 1)
                pe.wait_ge(x2T_copied, i + 1)
                if begun(i):
                    pe.wait_ge(rows_done, i)
                for t in range(TPP):
                    last = mm(gate_v[:, t, :], xn2T[:, t * P:(t + 1) * P], gate_w_sb[:, :], start=True, stop=True)
                last.then_inc(gate_done, 1)

            def rank(i):
                pe.wait_ge(chosen_done, i + 1)
                for t in range(TPP):
                    for s in range(t):
                        mm(rank_v[:, t, :], ones[:, :], chosen[:, s, :], start=(s == 0), stop=False)
                    mm(rank_v[:, t, :], before[:, :], chosen[:, t, :], start=(t == 0), stop=True)
                for t in range(TPP):
                    last = mm(total_v, ones[:, :], chosen[:, t, :], start=(t == 0), stop=(t == TPP - 1))
                last.then_inc(rank_done, 1)

            front(0)
            aggregate(0)
            front(1)
            aggregate(1)
            gate(0, 0, 2)
            with pe.Fori(0, (PAIRS - 2) // 2) as j:
                for s in range(2):
                    m = 2 * j + 2 + s
                    front(m)
                    rank(m - 2)
                    aggregate(m)
                    gate(m - 1, 1 - s, m + 1)
            rank(PAIRS - 2)
            gate(PAIRS - 1, 1, PAIRS)
            rank(PAIRS - 1)

            pe.wait_ge(table_cols, 1)
            mm(psum[0:1, 0, 0:P], blk[:, 3:4], ident[:, :], start=True, stop=True)
            mm(psum[0:1, 0, P:2 * P], blk[:, 6:7], ident[:, :], start=True, stop=True).then_inc(table_ps, 1)
            pe.wait_ge(table_done, 1)

            def turn_x(k, q, early):
                pe.wait_ge(block_in[q], 32 * (k + 1))
                if not early:
                    pe.wait_ge(xbT_done, k * RING + q - 1)
                for t in range(TPB):
                    last = tr(psum[:, q % 2, t * P:(t + 1) * P], xb[:, q, t, 0:D], ident[:, :])
                last.then_inc(xbT_ps_done, 1)

            def layer1(b, q, early):
                pe.wait_ge(xbT_done, b + 1)
                if not early:
                    pe.wait_ge(hid_done, b - 1)
                for c in range(FC):
                    last = mm(psum[:, 2 + q % 2, c * BT:(c + 1) * BT], wb[:, q, c * P:(c + 1) * P], xbT[:, q, :],
                              start=True, stop=True)
                last.then_inc(l1_done, 1)

            def layer2(b, q, early):
                pe.wait_ge(hid_done, b + 1)
                if not early:
                    pe.wait_ge(yb_done, b - 1)
                for t in range(TPB):
                    for c in range(FC):
                        last = mm(psum[:, 4 + q % 2, t * D:(t + 1) * D], hid[:, q, c, t * P:(t + 1) * P],
                                  wb[:, q, HID + c * D:HID + (c + 1) * D], start=(c == 0), stop=(c == FC - 1))
                last.then_inc(l2_done, 1)

            for q in range(RING):
                turn_x(0, q, q < 2)
                if q >= 1:
                    layer1(q - 1, q - 1, q - 1 < 2)
                if q >= 2:
                    layer2(q - 2, q - 2, True)
            with pe.Fori(1, BTURNS) as k:
                for q in range(RING):
                    b = k * RING + q
                    turn_x(k, q, False)
                    layer1(b - 1, (q - 1) % RING, False)
                    layer2(b - 2, (q - 2) % RING, False)
            layer1(NBLK - 1, RING - 1, False)
            layer2(NBLK - 2, RING - 2, False)
            layer2(NBLK - 1, RING - 1, False)


def kernel(x, adj, nodemask, L0_gnn_W, L0_gnn_b, L0_gnn_a1, L0_gnn_a2, L0_gnn_att_b, L0_ffn_gate_w, L0_ffn_gate_b,
           L0_ffn_w1, L0_ffn_b1, L0_ffn_w2, L0_ffn_b2, L0_ffn_gamma, L0_ffn_beta):
    import numpy as np
    import concourse.bacc as bacc
    from concourse.bass_utils import run_bass_kernel_spmd

    w1, w2 = np.asarray(L0_ffn_w1), np.asarray(L0_ffn_w2)
    b1, b2 = np.asarray(L0_ffn_b1), np.asarray(L0_ffn_b2)
    experts = np.concatenate([
        w1,
        w2.reshape(EXPERTS, FC, P, D).transpose(0, 2, 1, 3).reshape(EXPERTS, P, FC * D),
        b1.reshape(EXPERTS, FC, P).transpose(0, 2, 1),
        np.broadcast_to(b2[:, None, :], (EXPERTS, P, D)),
        np.broadcast_to(np.arange(EXPERTS, dtype=np.float32)[:, None, None], (EXPERTS, P, 1)),
    ], axis=2)
    arrays = dict(
        x=x, adj=adj, nodemask=nodemask, gnn_w=L0_gnn_W, gnn_b=L0_gnn_b, gnn_a1=L0_gnn_a1, gnn_a2=L0_gnn_a2,
        att_b=np.asarray(L0_gnn_att_b).reshape(1), gate_w=L0_ffn_gate_w, gate_b=L0_ffn_gate_b, experts=experts,
        gamma=L0_ffn_gamma, beta=L0_ffn_beta)
    arrays = {f"{name}_dram": np.ascontiguousarray(a) for name, a in arrays.items()}
    nc = bacc.Bacc("TRN2", target_bir_lowering=False, num_devices=1)
    args = [nc.dram_tensor(name, a.shape, F32, kind="ExternalInput").ap() for name, a in arrays.items()]
    out = nc.dram_tensor("out_dram", (GRAPHS, NODES, D), F32, kind="ExternalOutput").ap()
    build(nc, *args, out)
    return run_bass_kernel_spmd(nc, [arrays], core_ids=[0]).results[0]["out_dram"]
```

```python
from contextlib import ExitStack

import concourse.bass as bass
from concourse import mybir

F32 = mybir.dt.float32
BF16 = mybir.dt.bfloat16
I32 = mybir.dt.int32
U32 = mybir.dt.uint32
ALU = mybir.AluOpType
ACT = mybir.ActivationFunctionType
AX = mybir.AxisListType.X

P = 128
D = 128
GRAPHS, NODES = 32, 256
TPG = NODES // P
PAIRS = GRAPHS // 2
TPP = 2 * TPG
TILES = GRAPHS * TPG
TOKENS = GRAPHS * NODES
XCHUNKS = ((0, 4), (4, 16), (16, 32), (32, 48), (48, 64))
TPX = max(hi - lo for lo, hi in XCHUNKS)
EXPERTS, HID, TOPK = 16, 256, 2
FC = HID // P
BT = 256
TPB = BT // P
IN_RING = 8
RING = 4
NBLK = -(-(TOKENS * TOPK // BT + EXPERTS) // IN_RING) * IN_RING
BTURNS = NBLK // IN_RING
CAP = TOKENS + BT
PAD_ROW = EXPERTS * CAP
TO, WEIGHT, FIRST = D, D + 1, D + 2
RW = D + 3
B1, B2 = HID + FC * D, HID + FC * D + FC
WCOLS = B2 + D
HA = D + 2
GT = 4
GROUPS = TILES // GT
CRING = 4
CTURNS = GROUPS // CRING
DVE_FROM = 3
LOOP_FROM, LOOP_TO = 4, PAIRS - 2
SCATTERS = TPP * TOPK
EPS = 1e-5


def begun(turn, ago=1):
    return not isinstance(turn, int) or turn >= ago


def valid(pair):
    return not isinstance(pair, int) or 0 <= pair < PAIRS


def build(nc, x, adj, nodemask, gnn_w, gnn_b, gnn_a1, gnn_a2, att_b, gate_w, gate_b, experts, gamma, beta, out):
    ctx = ExitStack()
    with ctx:
        def sb(name, shape, dt=F32):
            return ctx.enter_context(nc.sbuf_tensor(name, shape, dt))

        def sem(name):
            return ctx.enter_context(nc.semaphore(name))

        sorted_x = nc.dram_tensor("sorted_x", (PAD_ROW + BT, RW), F32, kind="Internal").ap()
        token_y = nc.dram_tensor("token_y", (TOKENS * TOPK, D), F32, kind="Internal").ap()

        ident = sb("ident", [P, P])
        before = sb("before", [P, P], BF16)
        ones = sb("ones", [P, P], BF16)
        ones_f = sb("ones_f", [P, P])
        pad_rows = sb("pad_rows", [P, TPB, RW])
        result_row = sb("result_row", [P, TOPK, TILES])
        iota_e = sb("iota_e", [P, EXPERTS])
        iota_p = sb("iota_p", [P, 1])
        first_row = sb("first_row", [P, EXPERTS])
        neg_half = sb("neg_half", [P, TPX])
        eps_t = sb("eps_t", [P, 1])
        w_raw = sb("w_raw", [D, D])
        mask_rows = sb("mask_rows", [TILES, P])
        vec = sb("vec", [P, 4])
        a1_bc = sb("a1_bc", [P, P])
        w_aug = sb("w_aug", [P, HA])
        u1_bc = sb("u1_bc", [P, P])
        h_bias = sb("h_bias", [1, HA])
        att_b_sb = sb("att_b_sb", [1, 1])
        gate_w_sb = sb("gate_w_sb", [D, EXPERTS])
        gate_b_bc = sb("gate_b_bc", [P, EXPERTS])
        gamma_bc = sb("gamma_bc", [P, D])
        beta_bc = sb("beta_bc", [P, D])
        mask_t = sb("mask_t", [P, TILES])
        mask_sq = sb("mask_sq", [P, TILES])

        xmid = sb("xmid", [P, TILES, D])
        mv1 = sb("mv1", [P, TILES, 2])
        rs1 = sb("rs1", [P, TILES])
        rstd1 = sb("rstd1", [P, TILES])
        shift1 = sb("shift1", [P, 2, TILES])

        adj_in = sb("adj_in", [P, 2, TPG, NODES])
        st1 = sb("st1", [P, TPX, 6])
        xn = sb("xn", [P, TPP, D])
        xnT = sb("xnT", [P, TPP * P])
        h_sb = sb("h_sb", [P, 2, 2, TPG, HA])
        sig = sb("sig", [P, 2, TPG, NODES])
        att = sb("att", [P, 2, TPG, NODES])
        den = sb("den", [P, 4, 2, TPG])
        st2 = sb("st2", [P, TPP, 6])
        mv2 = sb("mv2", [P, TPP, 2])
        rs2 = sb("rs2", [P, 4, TPP])
        lead = sb("lead", [P, TPP])
        xrow = sb("xrow", [P, 2, TOPK, TPP, RW])
        xn2 = sb("xn2", [P, TPP, D])
        xn2T = sb("xn2T", [P, TPP * P])
        logits = sb("logits", [P, TPP, EXPERTS])
        m8 = sb("m8", [P, TPP, 8])
        i8 = sb("i8", [P, TPP, 8], U32)
        onehot = sb("onehot", [P, TPP, TOPK, EXPERTS])
        chosen = sb("chosen", [P, TPP, EXPERTS], BF16)
        count = sb("count", [P, EXPERTS])
        row_of = sb("row_of", [P, TPP, EXPERTS])
        picked = sb("picked", [P, TPP, TOPK, EXPERTS])
        rows = sb("rows", [P, 2, TPP, TOPK], I32)

        cnt_i = sb("cnt_i", [P, 2, EXPERTS], I32)
        nblk = sb("nblk", [P, EXPERTS])
        last_blk = sb("last_blk", [P, EXPERTS])
        past = sb("past", [P, 2, EXPERTS])
        blk = sb("blk", [P, 8])
        tab = sb("tab", [1, P], I32)
        fill_row = sb("fill_row", [P, EXPERTS], I32)

        xb = sb("xb", [P, IN_RING, TPB, RW])
        wb = sb("wb", [P, IN_RING, WCOLS])
        xbT = sb("xbT", [P, RING, BT])
        hid = sb("hid", [P, RING, FC, BT])
        yb = sb("yb", [P, RING, TPB, D])
        x_first = sb("x_first", [P, RING, TPB, D])
        y_row = sb("y_row", [P, RING, TPB], I32)

        got = sb("got", [P, CRING, GT, TOPK, D])
        y = sb("y", [P, CRING, GT, D])
        st3 = sb("st3", [P, CRING, GT, 6])
        mv3 = sb("mv3", [P, CRING, GT, 2])
        rs3 = sb("rs3", [P, CRING, 3, GT])
        z = sb("z", [P, CRING, GT, D])
        res = sb("res", [P, CRING, GT, D])

        psum = ctx.enter_context(nc.psum_tensor("psum", [P, 8, 512], F32))
        xT_ps, adjT_ps, h_ps, s1_ps, agg_ps, route_ps = (
            psum[:, 0, :], psum[:, 1:3, :], psum[:, 3, :], psum[:, 4, :], psum[:, 5:7, :], psum[:, 7, :])
        agg_v = agg_ps[:, :, 0:TPG * (D + 1)].rearrange("p g (t c) -> p g t c", c=D + 1)
        h_v = h_ps[:, 0:TPG * HA].rearrange("p (t c) -> p t c", c=HA)
        gate_v = route_ps[:, 0:TPP * EXPERTS].rearrange("p (t e) -> p t e", e=EXPERTS)
        rank_v = route_ps[:, TPP * EXPERTS:2 * TPP * EXPERTS].rearrange("p (t e) -> p t e", e=EXPERTS)
        total_v = route_ps[:, 2 * TPP * EXPERTS:(2 * TPP + 1) * EXPERTS]

        weights_in, consts_in, late_in = sem("weights_in"), sem("consts_in"), sem("late_in")
        const_done = sem("const_done")
        pool_step, dve_step = sem("pool_step"), sem("dve_step")
        setup_pe, setup_dve = sem("setup_pe"), sem("setup_dve")
        x_in = [sem(f"x_in{c}") for c in range(len(XCHUNKS))]
        adj_in_s = [sem(f"adj_in{p}") for p in range(2)]
        stats1, rstd1_done, xn_done = sem("stats1"), sem("rstd1_done"), sem("xn_done")
        xT_done, xT_copied = sem("xT_done"), sem("xT_copied")
        adjT_g, h_g, s1_done, h_sb_g, sig_g, att_g = (
            sem("adjT_g"), sem("h_g"), sem("s1_done"), sem("h_sb_g"), sem("sig_g"), sem("att_g"))
        agg_g, xmid_done = sem("agg_g"), sem("xmid_done")
        stats2, rstd2_done, xn2_done, xrow_done = sem("stats2"), sem("rstd2_done"), sem("xn2_done"), sem("xrow_done")
        x_kept = sem("x_kept")
        x2T_done, x2T_copied, gate_done = sem("x2T_done"), sem("x2T_copied"), sem("gate_done")
        chosen_done, rank_done, rows_done = sem("chosen_done"), sem("rank_done"), sem("rows_done")
        scattered = [sem(f"scattered{p}") for p in range(2)]
        fill_done, table_cols, table_ps, table_done, filled = (
            sem("fill_done"), sem("table_cols"), sem("table_ps"), sem("table_done"), sem("filled"))
        block_in = [sem(f"block_in{q}") for q in range(IN_RING)]
        xbT_ps_done, xbT_done, l1_done, hid_done, first_done, l2_done, yb_done = (
            sem("xbT_ps_done"), sem("xbT_done"), sem("l1_done"), sem("hid_done"), sem("first_done"), sem("l2_done"), sem("yb_done"))
        yb_out = [sem(f"yb_out{q}") for q in range(RING)]
        got_in = [sem(f"got_in{q}") for q in range(CRING)]
        added, y_done, std_done, shift_done, z_done, scaled, res_done = (
            sem("added"), sem("y_done"), sem("std_done"), sem("shift_done"), sem("z_done"), sem("scaled"), sem("res_done"))
        dve_added = sem("dve_added")
        res_out = [sem(f"res_out{q}") for q in range(CRING)]
        pool_passed, dve_passed, sp_passed = sem("pool_passed"), sem("dve_passed"), sem("sp_passed")

        def free_after(i, slot):
            return 16 * SCATTERS * ((i - slot) // 2)

        x_v = x.rearrange("g (t p) c -> p (g t) c", p=P)
        out_v = out.rearrange("g (t p) c -> p (g t) c", p=P)
        adj_v = adj.rearrange("g (t p) n -> g p t n", p=P)
        token_v = token_y.rearrange("(t p k) c -> p t k c", p=P, k=TOPK)
        block = ctx.enter_context(nc.Block())

        @block.sync
        def _(sp):
            for dst, src in ((w_raw[:, :], gnn_w), (vec[:, 0:1], gnn_a1.rearrange("(p a) -> p a", a=1)),
                             (vec[:, 1:2], gnn_a2.rearrange("(p a) -> p a", a=1)),
                             (vec[:, 2:3], gnn_b.rearrange("(p a) -> p a", a=1)),
                             (h_bias[:, 0:D], gnn_b.rearrange("(a c) -> a c", a=1)),
                             (att_b_sb[:, :], att_b.rearrange("(a c) -> a c", a=1))):
                sp.dma_start(dst, src).then_inc(weights_in, 16)
            sp.dma_start(mask_rows[:, :], nodemask.rearrange("g (t p) -> (g t) p", p=P)).then_inc(consts_in, 16)

            def load_adj(i):
                for p in range(2):
                    if begun(i):
                        sp.wait_ge(adjT_g, 2 * i + p - 1)
                    sp.dma_start(adj_in[:, p, :, :], adj_v[2 * i + p, :, :, :]).then_inc(adj_in_s[p], 16)

            load_adj(0)
            for dst, src in ((gate_w_sb[:, :], gate_w), (gate_b_bc[:, :], gate_b.partition_broadcast(P)),
                             (gamma_bc[:, :], gamma.partition_broadcast(P)),
                             (beta_bc[:, :], beta.partition_broadcast(P))):
                sp.dma_start(dst, src).then_inc(late_in, 16)
            with sp.Fori(1, PAIRS) as i:
                load_adj(i)

            sp.dma_start(sorted_x[PAD_ROW:PAD_ROW + BT, :].rearrange("(p t) c -> p t c", t=TPB),
                         pad_rows[:, :, :]).then_inc(filled, 16)
            sp.wait_ge(fill_done, 1)
            for e in range(0, EXPERTS, 2):
                row = sp.value_load(fill_row[0:1, e:e + 1], min_val=0, max_val=PAD_ROW - BT)
                sp.dma_start(sorted_x[bass.ds(row, BT), :].rearrange("(p t) c -> p t c", t=TPB),
                             pad_rows[:, :, :]).then_inc(filled, 16)
            sp.wait_ge(table_done, 1)

            def load_block(k, q):
                b = k * IN_RING + q
                entry = sp.value_load(tab[0:1, bass.ds(b, 1)], min_val=0, max_val=PAD_ROW * EXPERTS + EXPERTS - 1)
                e = (entry & (EXPERTS - 1)).with_bounds(min_val=0, max_val=EXPERTS - 1)
                row = (entry >> (EXPERTS.bit_length() - 1)).with_bounds(min_val=0, max_val=PAD_ROW)
                if begun(k):
                    sp.wait_ge(yb_done, b - IN_RING + 1)
                    sp.sem_inc(sp_passed, 1)
                sp.dma_start(wb[:, q, :], experts[bass.ds(e, 1), :, :].rearrange("a p c -> p (a c)")
                             ).then_inc(block_in[q], 16)
                if not begun(k) and q == 0:
                    sp.wait_ge(filled, 16 * (EXPERTS + 1))
                    sp.wait_ge(scattered[0], 16 * SCATTERS * PAIRS // 2)
                    sp.wait_ge(scattered[1], 16 * SCATTERS * PAIRS // 2)
                sp.dma_start(xb[:, q, :, :], sorted_x[bass.ds(row, BT), :].rearrange("(p t) c -> p t c", t=TPB)
                             ).then_inc(block_in[q], 16)

            for q in range(IN_RING):
                load_block(0, q)
            with sp.Fori(1, BTURNS) as k:
                for q in range(IN_RING):
                    load_block(k, q)

            for q in range(RING):
                sp.wait_ge(yb_out[q], 16 * TPB * NBLK // RING)

            def load_group(k, q):
                g = k * CRING + q
                if begun(k):
                    sp.wait_ge(added, g - CRING + 1)
                sp.dma_start(got[:, q, :, :, :], token_v[:, bass.ds(g * GT, GT), :, :]).then_inc(got_in[q], 16)

            for q in range(CRING):
                load_group(0, q)
            with sp.Fori(1, CTURNS) as k:
                for q in range(CRING):
                    load_group(k, q)
            for q in range(CRING):
                sp.wait_ge(res_out[q], 16 * CTURNS)

        @block.gpsimd
        def _(pool):
            g = nc.gpsimd
            g.memset(ident[:, :], 0.0).then_inc(pool_step, 1)
            g.memset(before[:, :], 1.0).then_inc(pool_step, 1)
            g.memset(pad_rows[:, :, :], 0.0).then_inc(pool_step, 1)
            g.memset(ones[:, :], 1.0).then_inc(const_done, 1)
            g.memset(ones_f[:, :], 1.0).then_inc(const_done, 1)
            g.memset(neg_half[:, :], -0.5).then_inc(const_done, 1)
            g.memset(eps_t[:, :], EPS).then_inc(const_done, 1)
            for k in range(TOPK):
                g.memset(xrow[:, :, k, :, FIRST], 1.0 - k).then_inc(const_done, 1)
            pool.wait_ge(pool_step, 3)
            g.affine_select(out=ident[:, :], in_=ident[:, :], compare_op=ALU.not_equal, fill=1.0, base=0,
                            pattern=[[-1, P]], channel_multiplier=1).then_inc(const_done, 1)
            g.affine_select(out=before[:, :], in_=before[:, :], compare_op=ALU.is_gt, fill=0.0, base=0,
                            pattern=[[1, P]], channel_multiplier=-1).then_inc(const_done, 1)
            for dst, pattern, base, by_partition in (
                    (iota_e[:, :], [[1, EXPERTS]], 0, 0), (iota_p[:, :], [[0, 1]], 0, 1),
                    (first_row[:, :], [[CAP, EXPERTS]], 0, 0), (result_row[:, :, :], [[1, TOPK], [2 * P, TILES]], 0, 2),
                    (pad_rows[:, :, TO], [[2, TPB]], 2 * TOKENS, 2 * TPB)):
                g.iota(dst, pattern=pattern, base=base, channel_multiplier=by_partition,
                       allow_small_or_imprecise_dtypes=True).then_inc(const_done, 1)

            def rstd1_of(c):
                lo, hi = XCHUNKS[c]
                pool.wait_ge(stats1, c + 1)
                g.tensor_scalar(rs1[:, lo:hi], mv1[:, lo:hi, 1], EPS, None, ALU.add).then_inc(pool_step, 1)
                g.tensor_scalar(shift1[:, 0, lo:hi], mv1[:, lo:hi, 0], -1.0, None, ALU.mult).then_inc(pool_step, 1)
                pool.wait_ge(pool_step, 3 + 3 * c + 2)
                g.tensor_tensor(rstd1[:, lo:hi], rs1[:, lo:hi], neg_half[:, 0:hi - lo], ALU.pow).then_inc(pool_step, 1)
                pool.wait_ge(pool_step, 3 + 3 * c + 3)
                g.tensor_tensor(shift1[:, 1, lo:hi], shift1[:, 0, lo:hi], rstd1[:, lo:hi], ALU.mult
                                ).then_inc(rstd1_done, (hi - lo) // TPP)

            def rstd2(i):
                if begun(i):
                    pool.wait_ge(xn2_done, i)
                pool.wait_ge(stats2, i + 1)
                g.tensor_tensor(rs2[:, 1, :], rs2[:, 0, :], neg_half[:, 0:TPP], ALU.pow).then_inc(pool_step, 1)
                pool.wait_ge(pool_step, 3 + 3 * len(XCHUNKS) + i + 1)
                g.tensor_tensor(rs2[:, 3, :], rs2[:, 2, :], rs2[:, 1, :], ALU.mult).then_inc(rstd2_done, 1)

            def scatter(slot, tiles):
                for t in tiles:
                    for k in range(TOPK):
                        pool.indirect_dma_start(
                            sorted_x, bass.IndirectOffsetOnAxis(ap=rows[:, slot, t, k:k + 1], axis=0),
                            xrow[:, slot, k, t, :], None).then_inc(scattered[slot], 16)

            def turn(m, slot):
                if valid(m - 3):
                    pool.wait_ge(xrow_done, m - 2)
                    pool.wait_ge(rows_done, m - 2)
                    pool.sem_inc(pool_passed, 1)
                    scatter(slot, range(TPP - 1))
                if valid(m - 1):
                    rstd2(m - 1)
                if valid(m - 3):
                    scatter(slot, range(TPP - 1, TPP))

            for c in range(len(XCHUNKS)):
                rstd1_of(c)
            for m in range(1, LOOP_FROM):
                turn(m, (m - 3) % 2)
            with pool.Fori(0, (LOOP_TO - LOOP_FROM) // 2) as j:
                for s in range(2):
                    turn(LOOP_FROM + 2 * j + s, (LOOP_FROM + s - 3) % 2)
            for m in range(LOOP_TO, PAIRS + 3):
                turn(m, (m - 3) % 2)

            with pool.Fori(0, NBLK // RING) as k:
                for q in range(RING):
                    pool.wait_ge(yb_done, k * RING + q + 1)
                    pool.sem_inc(pool_passed, 1)
                    for t in range(TPB):
                        pool.indirect_dma_start(
                            token_y, bass.IndirectOffsetOnAxis(ap=y_row[:, q, t:t + 1], axis=0), yb[:, q, t, :], None,
                            bounds_check=TOKENS * TOPK - 1, oob_is_err=False).then_inc(yb_out[q], 16)

            def finish(k, q):
                i = k * CRING + q
                pool.wait_ge(z_done, i + 1)
                g.tensor_tensor(z[:, q, :, :], z[:, q, :, :], gamma_bc[:, None, :].broadcast_to([P, GT, D]), ALU.mult
                                ).then_inc(scaled, 1)
                if begun(k):
                    pool.wait_ge(res_out[q], 16 * k)
                pool.wait_ge(scaled, i + 1)
                g.tensor_tensor(res[:, q, 0:DVE_FROM, :], z[:, q, 0:DVE_FROM, :], xmid[:, bass.ds(i * GT, DVE_FROM), :],
                                ALU.add).then_inc(res_done, 1)

            for q in range(CRING):
                finish(0, q)
            with pool.Fori(1, CTURNS) as k:
                for q in range(CRING):
                    finish(k, q)

        @block.scalar
        def _(act):
            for c, (lo, hi) in enumerate(XCHUNKS):
                if c == 1:
                    act.wait_ge(weights_in, 16 * 6)
                act.dma_start(xmid[:, lo:hi, :], x_v[:, lo:hi, :]).then_inc(x_in[c], 16)

            def norm1(i):
                act.wait_ge(rstd1_done, i + 1)
                if begun(i):
                    act.wait_ge(xT_done, i)
                for t in range(TPP):
                    tile = bass.ds(i * TPP + t, 1)
                    last = act.activation(xn[:, t, :], xmid[:, tile, :].rearrange("p a c -> p (a c)"), ACT.Identity,
                                          bias=shift1[:, 1, tile], scale=rstd1[:, tile])
                last.then_inc(xn_done, 1)

            def transposed2(i):
                act.wait_ge(x2T_done, i + 1)
                if begun(i):
                    act.wait_ge(gate_done, i)
                act.copy(xn2T[:, :], xT_ps).then_inc(x2T_copied, 1)

            def keep(i, slot):
                if begun(i, 2):
                    act.wait_ge(scattered[slot], free_after(i, slot))
                act.copy(xrow[:, slot, :, :, TO], result_row[:, :, bass.ds(i * TPP, TPP)])
                act.copy(xrow[:, slot, :, :, 0:D], xn2[:, None, :, :].broadcast_to([P, TOPK, TPP, D])).then_inc(x_kept, 1)

            def weigh(i, slot):
                act.wait_ge(chosen_done, i + 1)
                for k in range(TOPK):
                    last = act.activation(xrow[:, slot, k, :, WEIGHT], lead[:, :], ACT.Sigmoid, scale=1.0 - 2.0 * k)
                last.then_inc(xrow_done, 1)

            def transposed(i):
                act.wait_ge(xT_done, i + 1)
                if begun(i):
                    act.wait_ge(h_g, 2 * i)
                act.copy(xnT[:, :], xT_ps).then_inc(xT_copied, 1)

            def keep_h(i, p, slot):
                act.wait_ge(h_g, 2 * i + p + 1)
                if begun(i, 2):
                    act.wait_ge(agg_g, 2 * i + p - 3)
                act.copy(h_sb[:, slot, p, :, :], h_v).then_inc(h_sb_g, 1)

            def sigmoids(i, slot):
                act.wait_ge(s1_done, i + 1)
                for p in range(2):
                    act.wait_ge(h_sb_g, 2 * i + p + 1)
                    if begun(i):
                        act.wait_ge(att_g, 2 * i + p - 1)
                    for t in range(TPG):
                        last = act.activation(sig[:, p, t, :], s1_ps[:, p * NODES:(p + 1) * NODES], ACT.Sigmoid,
                                              bias=h_sb[:, slot, p, t, HA - 1:HA])
                    last.then_inc(sig_g, 1)

            def norm2(i):
                act.wait_ge(rstd2_done, i + 1)
                if begun(i):
                    act.wait_ge(x2T_done, i)
                    act.wait_ge(x_kept, i)
                for t in range(TPP):
                    last = act.activation(xn2[:, t, :], xmid[:, bass.ds(i * TPP + t, 1), :].rearrange("p a c -> p (a c)"),
                                          ACT.Identity, bias=rs2[:, 3, t:t + 1], scale=rs2[:, 1, t:t + 1])
                last.then_inc(xn2_done, 1)

            def turn(m, slot):
                if valid(m + 1):
                    keep_h(m + 1, 0, 1 - slot)
                if valid(m - 2):
                    transposed2(m - 2)
                if valid(m + 2):
                    norm1(m + 2)
                if valid(m + 1):
                    keep_h(m + 1, 1, 1 - slot)
                    sigmoids(m + 1, 1 - slot)
                if valid(m - 2):
                    keep(m - 2, slot)
                if valid(m + 2):
                    transposed(m + 2)
                if valid(m - 1):
                    norm2(m - 1)
                if valid(m - 2):
                    weigh(m - 2, slot)

            act.wait_ge(const_done, 13)
            norm1(0)
            transposed(0)
            for m in range(-1, LOOP_FROM):
                turn(m, m % 2)
            with act.Fori(0, (LOOP_TO - LOOP_FROM) // 2) as j:
                for s in range(2):
                    turn(LOOP_FROM + 2 * j + s, (LOOP_FROM + s) % 2)
            for m in range(LOOP_TO, PAIRS + 2):
                turn(m, m % 2)

            act.wait_ge(fill_done, 1)
            for e in range(1, EXPERTS, 2):
                row = act.value_load(fill_row[0:1, e:e + 1], min_val=0, max_val=PAD_ROW - BT)
                act.dma_start(sorted_x[bass.ds(row, BT), :].rearrange("(p t) c -> p t c", t=TPB),
                              pad_rows[:, :, :]).then_inc(filled, 16)

            def relu(k, q):
                b = k * IN_RING + q
                act.wait_ge(l1_done, b + 1)
                if begun(k) or q >= RING:
                    act.wait_ge(l2_done, b - RING + 1)
                for c in range(FC):
                    last = act.activation(hid[:, q % RING, c, :], psum[:, 2 + q % 2, c * BT:(c + 1) * BT], ACT.Relu,
                                          bias=wb[:, q, B1 + c:B1 + c + 1])
                last.then_inc(hid_done, 1)
                if begun(k) or q >= RING:
                    act.wait_ge(yb_done, b - RING + 1)
                for t in range(TPB):
                    last = act.activation(x_first[:, q % RING, t, :], xb[:, q, t, 0:D], ACT.Identity,
                                          scale=xb[:, q, t, FIRST:FIRST + 1])
                last.then_inc(first_done, 1)

            for q in range(IN_RING):
                relu(0, q)
            with act.Fori(1, BTURNS) as k:
                for q in range(IN_RING):
                    relu(k, q)

            def deviation(k, q):
                act.wait_ge(y_done, k * CRING + q + 1)
                act.activation(rs3[:, q, 0, :], mv3[:, q, :, 1], ACT.Sqrt, bias=eps_t[:, :]).then_inc(std_done, 1)

            def normalise(k, q):
                g = k * CRING + q
                act.wait_ge(shift_done, g + 1)
                if begun(k):
                    act.wait_ge(res_done, g - CRING + 1)
                    act.wait_ge(dve_added, g - CRING + 1)
                for t in range(GT):
                    last = act.activation(z[:, q, t, :], y[:, q, t, :], ACT.Identity, bias=rs3[:, q, 2, t:t + 1],
                                          scale=rs3[:, q, 1, t:t + 1])
                last.then_inc(z_done, 1)

            def store_group(k, q):
                g = k * CRING + q
                act.wait_ge(res_done, g + 1)
                act.wait_ge(dve_added, g + 1)
                act.dma_start(out_v[:, bass.ds(g * GT, GT), :], res[:, q, :, :]).then_inc(res_out[q], 16)

            for q in range(CRING):
                deviation(0, q)
                normalise(0, q)
            store_group(0, 0)
            with act.Fori(1, CTURNS) as k:
                for q in range(CRING):
                    deviation(k, q)
                    normalise(k, q)
                    if q < CRING - 1:
                        store_group(k - 1, q + 1)
                    else:
                        store_group(k, 0)
            for q in range(1, CRING):
                store_group(CTURNS - 1, q)

        @block.vector
        def _(dve):
            v = nc.vector
            steps = [0]

            def step(instruction):
                instruction.then_inc(dve_step, 1)
                steps[0] = steps[0] + 1
                return steps[0]

            def setup():
                dve.wait_ge(weights_in, 16 * 6)
                v.tensor_copy(a1_bc[:, :], vec[:, 0:1].broadcast_to([P, P])).then_inc(setup_dve, 1)
                v.tensor_tensor(vec[:, 3:4], vec[:, 0:1], vec[:, 1:2], ALU.add).then_inc(setup_dve, 1)
                v.memset(h_bias[:, D:D + 1], 1.0).then_inc(setup_dve, 1)
                v.memset(w_aug[:, D:D + 1], 0.0).then_inc(setup_dve, 1)
                dve.wait_ge(const_done, 13)
                step(v.tensor_copy(count[:, :], first_row[:, :]))
                dve.wait_ge(setup_pe, 1)
                n = step(v.tensor_copy(mask_t[:, :], psum[:, 1, 0:TILES]))
                v.tensor_copy(w_aug[:, 0:D], psum[:, 0, 0:P]).then_inc(setup_dve, 1)
                v.tensor_copy(w_aug[:, D + 1:D + 2], psum[:, 0, P:P + 1]).then_inc(setup_dve, 1)
                v.tensor_copy(u1_bc[:, :], psum[:, 0, 2 * P:3 * P]).then_inc(setup_dve, 1)
                v.tensor_tensor(h_bias[:, D + 1:D + 2], psum[0:1, 0, P + 1:P + 2], att_b_sb[:, :], ALU.add
                                ).then_inc(setup_dve, 1)
                dve.wait_ge(dve_step, n)
                step(v.tensor_tensor(mask_sq[:, :], mask_t[:, :], mask_t[:, :], ALU.mult))

            def stats_of(c):
                lo, hi = XCHUNKS[c]
                dve.wait_ge(x_in[c], 16)
                if c:
                    dve.wait_ge(stats1, c)
                for t in range(lo, hi):
                    n = step(v.bn_stats(st1[:, t - lo, :], xmid[:, t, :]))
                dve.wait_ge(dve_step, n)
                for t in range(lo, hi):
                    last = v.bn_aggr(mv1[:, t, :], st1[:, t - lo, :])
                last.then_inc(stats1, 1)

            def attend(i, p, t):
                if t == 0:
                    dve.wait_ge(adjT_g, 2 * i + p + 1)
                    dve.wait_ge(sig_g, 2 * i + p + 1)
                    if begun(i):
                        dve.wait_ge(agg_g, 2 * i + p - 1)
                last = v.scalar_tensor_tensor(
                    out=att[:, p, t, :], in0=adjT_ps[:, p, t * NODES:(t + 1) * NODES],
                    scalar=mask_t[:, bass.ds((2 * i + p) * TPG + t, 1)], in1=sig[:, p, t, :], op0=ALU.mult, op1=ALU.mult)
                if t == TPG - 1:
                    last.then_inc(att_g, 1)

            def by_graph(cols, i):
                return cols[:, bass.ds(i * TPP, TPP)].rearrange("p (g t) -> p g t", t=TPG)

            def attention_and_residual(m):
                i, res, now = m - 1, valid(m - 1), valid(m)
                if res:
                    dve.wait_ge(agg_g, 2 * i + 2)
                    n = step(v.tensor_tensor(den[:, 0, :, :], agg_v[:, :, :, D], by_graph(mask_t, i), ALU.mult))
                if now:
                    attend(m, 0, 0)
                if res:
                    dve.wait_ge(dve_step, n)
                    n = step(v.tensor_scalar(den[:, 1, :, :], den[:, 0, :, :], 1e-8, None, ALU.add))
                if now:
                    attend(m, 0, 1)
                if res:
                    dve.wait_ge(dve_step, n)
                    n = step(v.reciprocal(den[:, 2, :, :], den[:, 1, :, :]))
                if now:
                    attend(m, 1, 0)
                if res:
                    dve.wait_ge(dve_step, n)
                    n = step(v.tensor_tensor(den[:, 3, :, :], den[:, 2, :, :], by_graph(mask_sq, i), ALU.mult))
                if now:
                    attend(m, 1, 1)
                if res:
                    dve.wait_ge(dve_step, n)
                    for t in range(TPP):
                        row = xmid[:, bass.ds(i * TPP + t, 1), :].rearrange("p a c -> p (a c)")
                        ins = v.scalar_tensor_tensor(out=row, in0=agg_v[:, t // TPG, t % TPG, 0:D],
                                                     scalar=den[:, 3, t // TPG, t % TPG:t % TPG + 1],
                                                     in1=row, op0=ALU.mult, op1=ALU.add)
                    ins.then_inc(xmid_done, 1)

            def variance(i):
                dve.wait_ge(xmid_done, i + 1)
                dve.sem_inc(dve_passed, 1)
                for t in range(TPP):
                    n = step(v.bn_stats(st2[:, t, :], xmid[:, bass.ds(i * TPP + t, 1), :].rearrange("p a c -> p (a c)")))
                dve.wait_ge(dve_step, n)
                dve.sem_inc(dve_passed, 1)
                for t in range(TPP):
                    n = step(v.bn_aggr(mv2[:, t, :], st2[:, t, :]))
                dve.wait_ge(dve_step, n)
                if begun(i):
                    dve.wait_ge(rstd2_done, i)
                v.tensor_scalar(rs2[:, 2, :], mv2[:, :, 0], -1.0, None, ALU.mult)
                v.tensor_scalar(rs2[:, 0, :], mv2[:, :, 1], EPS, None, ALU.add).then_inc(stats2, 1)

            def route(i):
                dve.wait_ge(gate_done, i + 1)
                n = step(v.tensor_tensor(logits[:, :, :], gate_v, gate_b_bc[:, None, :].broadcast_to([P, TPP, EXPERTS]),
                                         ALU.add))
                dve.wait_ge(dve_step, n)
                dve.sem_inc(dve_passed, 1)
                for t in range(TPP):
                    n = step(v.max(m8[:, t, :], logits[:, t, :]))
                dve.wait_ge(dve_step, n)
                dve.sem_inc(dve_passed, 1)
                for t in range(TPP):
                    n = step(v.max_index(i8[:, t, :], m8[:, t, :], logits[:, t, :]))
                if begun(i):
                    dve.wait_ge(xrow_done, i)
                v.tensor_tensor(lead[:, :], m8[:, :, 0], m8[:, :, 1], ALU.subtract)
                dve.wait_ge(dve_step, n)
                n = step(v.tensor_tensor(
                    onehot[:, :, :, :],
                    i8[:, :, 0:TOPK].rearrange("p t (k a) -> p t k a", a=1).broadcast_to([P, TPP, TOPK, EXPERTS]),
                    iota_e[:, None, None, :].broadcast_to([P, TPP, TOPK, EXPERTS]), ALU.is_equal))
                dve.wait_ge(dve_step, n)
                v.tensor_tensor(chosen[:, :, :], onehot[:, :, 0, :], onehot[:, :, 1, :], ALU.add).then_inc(chosen_done, 1)

            def place(i, slot):
                dve.wait_ge(rank_done, i + 1)
                n = step(v.tensor_tensor(row_of[:, :, :], rank_v, count[:, None, :].broadcast_to([P, TPP, EXPERTS]), ALU.add))
                dve.wait_ge(dve_step, n)
                step(v.tensor_tensor(count[:, :], count[:, :], total_v, ALU.add))
                n = step(v.tensor_tensor(picked[:, :, :, :], onehot[:, :, :, :],
                                         row_of[:, :, None, :].broadcast_to([P, TPP, TOPK, EXPERTS]), ALU.mult))
                if begun(i, 2):
                    dve.wait_ge(scattered[slot], free_after(i, slot))
                dve.wait_ge(dve_step, n)
                with nc.allow_low_precision(reason="whole numbers below 2**24 are summed in float32, then stored as int32"):
                    v.tensor_reduce(rows[:, slot, :, :], picked[:, :, :, :], axis=AX, op=ALU.add).then_inc(rows_done, 1)

            def turn(m, slot):
                attention_and_residual(m)
                if valid(m - 1):
                    variance(m - 1)
                if valid(m - 2):
                    route(m - 2)
                if valid(m - 2):
                    place(m - 2, slot)

            stats_of(0)
            setup()
            for c in range(1, len(XCHUNKS) - 1):
                stats_of(c)
            turn(0, 0)
            stats_of(len(XCHUNKS) - 1)
            turn(1, 1)
            per = steps[0]
            turn(2, 0)
            per = steps[0] - per
            turn(3, 1)
            base = steps[0]
            with dve.Fori(0, (LOOP_TO - LOOP_FROM) // 2) as j:
                for s in range(2):
                    steps[0] = base + j * (2 * per) + s * per
                    turn(LOOP_FROM + 2 * j + s, (LOOP_FROM + s) % 2)
            steps[0] = base + per * (LOOP_TO - LOOP_FROM)
            for m in range(LOOP_TO, PAIRS + 2):
                turn(m, m % 2)

            dve.wait_ge(dve_step, steps[0])
            v.tensor_copy(fill_row[:, :], count[:, :]).then_inc(fill_done, 1)
            n = step(v.scalar_tensor_tensor(out=past[:, 0, :], in0=count[:, :], scalar=float(BT - 1), in1=first_row[:, :],
                                            op0=ALU.add, op1=ALU.subtract))
            dve.wait_ge(dve_step, n)
            n = step(v.tensor_copy(cnt_i[:, 0, :], past[:, 0, :]))
            dve.wait_ge(dve_step, n)
            n = step(v.tensor_scalar(cnt_i[:, 1, :], cnt_i[:, 0, :], BT.bit_length() - 1, None, ALU.arith_shift_right))
            dve.wait_ge(dve_step, n)
            n = step(v.tensor_copy(nblk[:, :], cnt_i[:, 1, :]))
            dve.wait_ge(dve_step, n)
            n = step(v.tensor_tensor_scan(last_blk[:, :], ones_f[:, 0:EXPERTS], nblk[:, :], 0.0, ALU.mult, ALU.add))
            dve.wait_ge(dve_step, n)
            n = step(v.tensor_scalar(past[:, 0, :], last_blk[:, :], iota_p[:, :], None, ALU.is_le))
            dve.wait_ge(dve_step, n)
            step(v.tensor_reduce(blk[:, 0:1], past[:, 0, :], axis=AX, op=ALU.add))
            n = step(v.tensor_tensor(past[:, 1, :], past[:, 0, :], nblk[:, :], ALU.mult))
            dve.wait_ge(dve_step, n)
            n = step(v.tensor_reduce(blk[:, 1:2], past[:, 1, :], axis=AX, op=ALU.add))
            dve.wait_ge(dve_step, n)
            step(v.tensor_scalar(blk[:, 3:4], blk[:, 0:1], float(EXPERTS - 1), None, ALU.min))
            step(v.tensor_scalar(blk[:, 4:5], blk[:, 0:1], float(EXPERTS), None, ALU.is_lt))
            n = step(v.tensor_tensor(blk[:, 2:3], iota_p[:, :], blk[:, 1:2], ALU.subtract))
            dve.wait_ge(dve_step, n)
            n = step(v.scalar_tensor_tensor(out=blk[:, 5:6], in0=blk[:, 2:3], scalar=float(BT), in1=blk[:, 4:5],
                                            op0=ALU.mult, op1=ALU.mult))
            dve.wait_ge(dve_step, n)
            n = step(v.scalar_tensor_tensor(out=blk[:, 6:7], in0=blk[:, 0:1], scalar=float(CAP), in1=blk[:, 5:6],
                                            op0=ALU.mult, op1=ALU.add))
            dve.wait_ge(dve_step, n)
            v.scalar_tensor_tensor(out=blk[:, 7:8], in0=blk[:, 6:7], scalar=float(EXPERTS), in1=blk[:, 3:4],
                                   op0=ALU.mult, op1=ALU.add).then_inc(table_cols, 1)
            dve.wait_ge(table_ps, 1)
            v.tensor_copy(tab[:, :], psum[0:1, 0, 0:P]).then_inc(table_done, 1)

            def block_x(k, q):
                b, h = k * IN_RING + q, q % RING
                dve.wait_ge(xbT_ps_done, b + 1)
                if begun(k) or q >= RING:
                    dve.wait_ge(l1_done, b - RING + 1)
                v.tensor_copy(xbT[:, h, :], psum[:, q % 2, 0:BT]).then_inc(xbT_done, 1)

            def block_y(b, q, earlier):
                h = q % RING
                if begun(earlier):
                    dve.wait_ge(yb_out[h], 16 * TPB * earlier)
                dve.wait_ge(l2_done, b + 1)
                n = step(v.tensor_tensor(
                    yb[:, h, :, :], psum[:, 4 + q % 2, 0:TPB * D].rearrange("p (t c) -> p t c", c=D),
                    wb[:, q, None, B2:B2 + D].broadcast_to([P, TPB, D]), ALU.add))
                v.tensor_copy(y_row[:, h, :], xb[:, q, :, TO])
                dve.wait_ge(first_done, b + 1)
                dve.wait_ge(dve_step, n)
                for t in range(TPB):
                    last = v.scalar_tensor_tensor(out=yb[:, h, t, :], in0=yb[:, h, t, :],
                                                  scalar=xb[:, q, t, WEIGHT:WEIGHT + 1],
                                                  in1=x_first[:, h, t, :], op0=ALU.mult, op1=ALU.add)
                last.then_inc(yb_done, 1)

            def add_beta(k):
                tiles = xmid[:, bass.ds(k * GT, GT), :]
                v.tensor_tensor(tiles, tiles, beta_bc[:, None, :].broadcast_to([P, GT, D]), ALU.add)

            base = steps[0]

            def turn_b(k, q):
                block_x(k, q)
                b = k * IN_RING + q - 2
                steps[0] = base + b
                block_y(b, (q - 2) % IN_RING, k * (IN_RING // RING) + (q - 2) // RING)

            block_x(0, 0)
            block_x(0, 1)
            for q in range(2, IN_RING):
                turn_b(0, q)
            with dve.Fori(1, 1 + GROUPS // 2) as k:
                for q in range(IN_RING):
                    turn_b(k, q)
                    if q % (IN_RING // 2) == 0:
                        add_beta(2 * (k - 1) + q // (IN_RING // 2))
            for k in range(1 + GROUPS // 2, BTURNS):
                for q in range(IN_RING):
                    turn_b(k, q)
            steps[0] = base + NBLK - 2
            for b in (NBLK - 2, NBLK - 1):
                block_y(b, b % IN_RING, b // RING)

            def add(k, q):
                dve.wait_ge(got_in[q], 16 * (k + 1))
                if begun(k):
                    dve.wait_ge(z_done, k * CRING + q - CRING + 1)
                v.tensor_tensor(y[:, q, :, :], got[:, q, :, 0, :], got[:, q, :, 1, :], ALU.add).then_inc(added, 1)

            def aggregate(q):
                for t in range(GT):
                    last = v.bn_aggr(mv3[:, q, t, :], st3[:, q, t, :])
                last.then_inc(y_done, 1)

            def stats(k, q):
                dve.wait_ge(added, k * CRING + q + 1)
                dve.sem_inc(dve_passed, 1)
                for t in range(GT):
                    step(v.bn_stats(st3[:, q, t, :], y[:, q, t, :]))

            def shift(g, q):
                dve.wait_ge(std_done, g + 1)
                n = step(v.reciprocal(rs3[:, q, 1, :], rs3[:, q, 0, :]))
                dve.wait_ge(dve_step, n)
                v.scalar_tensor_tensor(out=rs3[:, q, 2, :], in0=mv3[:, q, :, 0], scalar=-1.0, in1=rs3[:, q, 1, :],
                                       op0=ALU.mult, op1=ALU.mult).then_inc(shift_done, 1)

            def finish(k, q):
                g = k * CRING + q
                dve.wait_ge(scaled, g + 1)
                if begun(k):
                    dve.wait_ge(res_out[q], 16 * k)
                v.tensor_tensor(res[:, q, DVE_FROM:GT, :], z[:, q, DVE_FROM:GT, :],
                                xmid[:, bass.ds(g * GT + DVE_FROM, GT - DVE_FROM), :], ALU.add).then_inc(dve_added, 1)

            def turn_c(k, q):
                last_q = (q - 1) % CRING
                n = steps[0]
                add(k, q)
                dve.wait_ge(dve_step, n)
                dve.sem_inc(dve_passed, 1)
                aggregate(last_q)
                stats(k, q)
                shift(k * CRING + q - 1, last_q)

            add(0, 0)
            stats(0, 0)
            for q in range(1, CRING):
                turn_c(0, q)
            finish(0, 0)
            base, per = steps[0], GT + 1
            with dve.Fori(1, CTURNS) as k:
                for q in range(CRING):
                    steps[0] = base + ((k - 1) * CRING + q) * per
                    turn_c(k, q)
                    if q < CRING - 1:
                        finish(k - 1, q + 1)
                    else:
                        finish(k, 0)
            dve.wait_ge(dve_step, base + (GROUPS - CRING) * per)
            aggregate(CRING - 1)
            steps[0] = base + (GROUPS - CRING) * per
            shift(GROUPS - 1, CRING - 1)
            for q in range(1, CRING):
                finish(CTURNS - 1, q)

        @block.tensor
        def _(pe):
            mm, tr = nc.tensor.matmul, nc.tensor.transpose

            pe.wait_ge(const_done, 13)
            pe.wait_ge(setup_dve, 4)
            tr(psum[:, 0, 0:P], w_raw[:, :], ident[:, :])
            mm(psum[:, 0, P:P + 1], w_raw[:, :], vec[:, 1:2], start=True, stop=True)
            mm(psum[0:1, 0, P + 1:P + 2], vec[:, 2:3], vec[:, 3:4], start=True, stop=True)
            mm(psum[:, 0, 2 * P:3 * P], w_raw[:, :], a1_bc[:, :], start=True, stop=True)
            pe.wait_ge(consts_in, 16)
            tr(psum[:, 1, 0:TILES], mask_rows[:, :], ident[0:TILES, 0:TILES]).then_inc(setup_pe, 1)
            pe.wait_ge(setup_dve, 8)

            def transpose_x(i):
                pe.wait_ge(xn_done, i + 1)
                if begun(i, 4):
                    pe.wait_ge(x2T_copied, i - 3)
                for t in range(TPP):
                    last = tr(xT_ps[:, t * P:(t + 1) * P], xn[:, t, :], ident[:, :])
                last.then_inc(xT_done, 1)

            def transpose_adj(i):
                for p in range(2):
                    pe.wait_ge(adj_in_s[p], 16 * (i + 1))
                    if begun(i):
                        pe.wait_ge(att_g, 2 * i + p - 1)
                    for jt in range(TPG):
                        for it in range(TPG):
                            last = tr(adjT_ps[:, p, jt * NODES + it * P:jt * NODES + (it + 1) * P],
                                      adj_in[:, p, it, jt * P:(jt + 1) * P], ident[:, :])
                    last.then_inc(adjT_g, 1)

            def project(i, p):
                if p == 0:
                    pe.wait_ge(xT_copied, i + 1)
                if begun(i) or p:
                    pe.wait_ge(h_sb_g, 2 * i + p)
                for t in range(TPG):
                    c = (p * TPG + t) * P
                    mm(h_v[:, t, :], xnT[:, c:c + P], w_aug[:, :], start=True, stop=False)
                    last = mm(h_v[:, t, :], ones_f[0:1, :], h_bias[:, :], start=False, stop=True)
                last.then_inc(h_g, 1)

            def project_s1(i):
                if begun(i):
                    pe.wait_ge(sig_g, 2 * i)
                mm(s1_ps, u1_bc[:, :], xnT[:, :], start=True, stop=True).then_inc(s1_done, 1)

            def aggregate(i, slot):
                if begun(i):
                    pe.wait_ge(xmid_done, i)
                for p in range(2):
                    pe.wait_ge(h_sb_g, 2 * i + p + 1)
                    pe.wait_ge(att_g, 2 * i + p + 1)
                    for it in range(TPG):
                        for jt in range(TPG):
                            last = mm(agg_v[:, p, it, :], att[:, p, jt, it * P:(it + 1) * P], h_sb[:, slot, p, jt, 0:D + 1],
                                      start=(jt == 0), stop=(jt == TPG - 1))
                    last.then_inc(agg_g, 1)

            def transpose_x2(i, fronts):
                pe.wait_ge(xn2_done, i + 1)
                pe.wait_ge(xT_copied, fronts)
                for t in range(TPP):
                    last = tr(xT_ps[:, t * P:(t + 1) * P], xn2[:, t, :], ident[:, :])
                last.then_inc(x2T_done, 1)

            def gate(i):
                if not begun(i):
                    pe.wait_ge(late_in, 16 * 4)
                pe.wait_ge(x2T_copied, i + 1)
                if begun(i):
                    pe.wait_ge(rows_done, i)
                for t in range(TPP):
                    last = mm(gate_v[:, t, :], xn2T[:, t * P:(t + 1) * P], gate_w_sb[:, :], start=True, stop=True)
                last.then_inc(gate_done, 1)

            def rank(i):
                pe.wait_ge(chosen_done, i + 1)
                for t in range(TPP):
                    for s in range(t):
                        mm(rank_v[:, t, :], ones[:, :], chosen[:, s, :], start=(s == 0), stop=False)
                    mm(rank_v[:, t, :], before[:, :], chosen[:, t, :], start=(t == 0), stop=True)
                for t in range(TPP):
                    last = mm(total_v, ones[:, :], chosen[:, t, :], start=(t == 0), stop=(t == TPP - 1))
                last.then_inc(rank_done, 1)

            def turn(m, slot):
                if valid(m + 1):
                    project(m + 1, 0)
                if valid(m - 2):
                    transpose_x2(m - 2, m + 2 if not isinstance(m, int) else min(m + 2, PAIRS))
                if valid(m + 1):
                    project_s1(m + 1)
                    project(m + 1, 1)
                if valid(m - 2):
                    gate(m - 2)
                if valid(m):
                    aggregate(m, slot)
                if valid(m - 2):
                    rank(m - 2)
                if valid(m + 2):
                    transpose_x(m + 2)
                if valid(m + 1):
                    transpose_adj(m + 1)

            transpose_x(0)
            for m in range(-1, LOOP_FROM):
                turn(m, m % 2)
            with pe.Fori(0, (LOOP_TO - LOOP_FROM) // 2) as j:
                for s in range(2):
                    turn(LOOP_FROM + 2 * j + s, (LOOP_FROM + s) % 2)
            for m in range(LOOP_TO, PAIRS + 2):
                turn(m, m % 2)

            pe.wait_ge(table_cols, 1)
            mm(psum[0:1, 0, 0:P], blk[:, 7:8], ident[:, :], start=True, stop=True).then_inc(table_ps, 1)
            pe.wait_ge(table_done, 1)

            def turn_x(k, q, early):
                pe.wait_ge(block_in[q], 32 * (k + 1))
                if not early:
                    pe.wait_ge(xbT_done, k * IN_RING + q - 1)
                for t in range(TPB):
                    last = tr(psum[:, q % 2, t * P:(t + 1) * P], xb[:, q, t, 0:D], ident[:, :])
                last.then_inc(xbT_ps_done, 1)

            def layer1(b, q, early):
                pe.wait_ge(xbT_done, b + 1)
                if not early:
                    pe.wait_ge(hid_done, b - 1)
                for c in range(FC):
                    last = mm(psum[:, 2 + q % 2, c * BT:(c + 1) * BT], wb[:, q, c * P:(c + 1) * P], xbT[:, q % RING, :],
                              start=True, stop=True)
                last.then_inc(l1_done, 1)

            def layer2(b, q, early):
                pe.wait_ge(hid_done, b + 1)
                if not early:
                    pe.wait_ge(yb_done, b - 1)
                for t in range(TPB):
                    for c in range(FC):
                        last = mm(psum[:, 4 + q % 2, t * D:(t + 1) * D], hid[:, q % RING, c, t * P:(t + 1) * P],
                                  wb[:, q, HID + c * D:HID + (c + 1) * D], start=(c == 0), stop=(c == FC - 1))
                last.then_inc(l2_done, 1)

            for q in range(IN_RING):
                turn_x(0, q, q < 2)
                if q >= 1:
                    layer1(q - 1, q - 1, q - 1 < 2)
                if q >= 2:
                    layer2(q - 2, q - 2, q - 2 < 2)
            with pe.Fori(1, BTURNS) as k:
                for q in range(IN_RING):
                    b = k * IN_RING + q
                    turn_x(k, q, False)
                    layer1(b - 1, (q - 1) % IN_RING, False)
                    layer2(b - 2, (q - 2) % IN_RING, False)
            layer1(NBLK - 1, IN_RING - 1, False)
            layer2(NBLK - 2, IN_RING - 2, False)
            layer2(NBLK - 1, IN_RING - 1, False)


def kernel(x, adj, nodemask, L0_gnn_W, L0_gnn_b, L0_gnn_a1, L0_gnn_a2, L0_gnn_att_b, L0_ffn_gate_w, L0_ffn_gate_b,
           L0_ffn_w1, L0_ffn_b1, L0_ffn_w2, L0_ffn_b2, L0_ffn_gamma, L0_ffn_beta):
    import numpy as np
    import concourse.bacc as bacc
    from concourse.bass_utils import run_bass_kernel_spmd

    w1, w2 = np.asarray(L0_ffn_w1), np.asarray(L0_ffn_w2)
    b1, b2 = np.asarray(L0_ffn_b1), np.asarray(L0_ffn_b2)
    experts = np.concatenate([
        w1,
        w2.reshape(EXPERTS, FC, P, D).transpose(0, 2, 1, 3).reshape(EXPERTS, P, FC * D),
        b1.reshape(EXPERTS, FC, P).transpose(0, 2, 1),
        np.broadcast_to(b2[:, None, :], (EXPERTS, P, D)),
    ], axis=2)
    arrays = dict(
        x=x, adj=adj, nodemask=nodemask, gnn_w=L0_gnn_W, gnn_b=L0_gnn_b, gnn_a1=L0_gnn_a1, gnn_a2=L0_gnn_a2,
        att_b=np.asarray(L0_gnn_att_b).reshape(1), gate_w=L0_ffn_gate_w, gate_b=L0_ffn_gate_b, experts=experts,
        gamma=L0_ffn_gamma, beta=L0_ffn_beta)
    arrays = {f"{name}_dram": np.ascontiguousarray(a) for name, a in arrays.items()}
    nc = bacc.Bacc("TRN2", target_bir_lowering=False, num_devices=1)
    args = [nc.dram_tensor(name, a.shape, F32, kind="ExternalInput").ap() for name, a in arrays.items()]
    out = nc.dram_tensor("out_dram", (GRAPHS, NODES, D), F32, kind="ExternalOutput").ap()
    build(nc, *args, out)
    return run_bass_kernel_spmd(nc, [arrays], core_ids=[0]).results[0]["out_dram"]
```

```python
from contextlib import ExitStack

import concourse.bass as bass
from concourse import mybir

F32 = mybir.dt.float32
BF16 = mybir.dt.bfloat16
I32 = mybir.dt.int32
U32 = mybir.dt.uint32
ALU = mybir.AluOpType
ACT = mybir.ActivationFunctionType
AX = mybir.AxisListType.X

P = 128
D = 128
GRAPHS, NODES = 32, 256
TPG = NODES // P
PAIRS = GRAPHS // 2
RSQRT_BITS = 0x5F3759DF
TPP = 2 * TPG
TILES = GRAPHS * TPG
TOKENS = GRAPHS * NODES
XCHUNKS = ((0, 4), (4, 16), (16, 32), (32, 48), (48, 64))
TPX = max(hi - lo for lo, hi in XCHUNKS)
EXPERTS, HID, TOPK = 16, 256, 2
assert EXPERTS == PAIRS
FC = HID // P
BT = 256
TPB = BT // P
IN_RING = 8
RING = 4
NBLK = -(-(TOKENS * TOPK // BT + EXPERTS) // IN_RING) * IN_RING
BTURNS = NBLK // IN_RING
CAP = TOKENS + BT
PAD_ROW = EXPERTS * CAP
TO, WEIGHT, FIRST = D, D + 1, D + 2
RW = D + 3
B1, B2, W2 = HID, HID + FC, HID + FC + D
WCOLS = W2 + FC * D
HA = D + 2
GT = 4
GROUPS = TILES // GT
CRING = 4
CTURNS = GROUPS // CRING
DVE_FROM = 3
LOOP_FROM, LOOP_TO = 4, PAIRS - 2
SCATTERS = TPP * TOPK
EPS = 1e-5


def begun(turn, ago=1):
    return not isinstance(turn, int) or turn >= ago


def valid(pair):
    return not isinstance(pair, int) or 0 <= pair < PAIRS


def build(nc, x, adj, nodemask, gnn_w, gnn_b, gnn_a1, gnn_a2, att_b, gate_w, gate_b, experts, gamma, beta, out):
    ctx = ExitStack()
    with ctx:
        def sb(name, shape, dt=F32):
            return ctx.enter_context(nc.sbuf_tensor(name, shape, dt))

        def sem(name):
            return ctx.enter_context(nc.semaphore(name))

        sorted_x = nc.dram_tensor("sorted_x", (PAD_ROW + BT, RW), F32, kind="Internal").ap()
        token_y = nc.dram_tensor("token_y", (TOKENS * TOPK, D), F32, kind="Internal").ap()

        ident = sb("ident", [P, P])
        before = sb("before", [P, P], BF16)
        ones = sb("ones", [P, P], BF16)
        ones_f = sb("ones_f", [P, P])
        pad_rows = sb("pad_rows", [P, TPB, RW])
        result_row = sb("result_row", [P, TOPK, TILES])
        iota_e = sb("iota_e", [P, EXPERTS])
        iota_p = sb("iota_p", [P, 1])
        first_row = sb("first_row", [P, EXPERTS])
        neg_half = sb("neg_half", [P, TPX])
        eps_t = sb("eps_t", [P, 1])
        w_raw = sb("w_raw", [D, D])
        mask_rows = sb("mask_rows", [TILES, P])
        vec = sb("vec", [P, 4])
        a1_bc = sb("a1_bc", [P, P])
        w_aug = sb("w_aug", [P, HA])
        u1_bc = sb("u1_bc", [P, P])
        h_bias = sb("h_bias", [1, HA])
        att_b_sb = sb("att_b_sb", [1, 1])
        gate_w_sb = sb("gate_w_sb", [D, EXPERTS])
        gate_b_bc = sb("gate_b_bc", [P, EXPERTS])
        gamma_bc = sb("gamma_bc", [P, D])
        beta_bc = sb("beta_bc", [P, D])
        mask_t = sb("mask_t", [P, TILES])
        mask_sq = sb("mask_sq", [P, TILES])

        xmid = sb("xmid", [P, TILES, D])
        mv1 = sb("mv1", [P, TILES, 2])
        rs1 = sb("rs1", [P, TILES])
        rstd1 = sb("rstd1", [P, TILES])
        shift1 = sb("shift1", [P, 2, TILES])

        adj_in = sb("adj_in", [P, 2, TPG, NODES])
        st1 = sb("st1", [P, TPX, 6])
        xn = sb("xn", [P, TPP, D])
        xnT = sb("xnT", [P, TPP * P])
        h_sb = sb("h_sb", [P, 2, 2, TPG, HA])
        sig = sb("sig", [P, 2, TPG, NODES])
        att = sb("att", [P, 2, TPG, NODES])
        den = sb("den", [P, 4, 2, TPG])
        st2 = sb("st2", [P, TPP, 6])
        mv2 = sb("mv2", [P, TPP, 2])
        rs2 = sb("rs2", [P, 2, TPP])
        var_eps = sb("var_eps", [P, 2, TPP])
        bits = sb("bits", [P, 2, TPP], I32)
        newton = sb("newton", [P, 4, TPP])
        lead = sb("lead", [P, TPP])
        xrow = sb("xrow", [P, 2, TOPK, TPP, RW])
        xn2 = sb("xn2", [P, TPP, D])
        xn2T = sb("xn2T", [P, TPP * P])
        logits = sb("logits", [P, TPP, EXPERTS])
        m8 = sb("m8", [P, TPP, 8])
        i8 = sb("i8", [P, TPP, 8], U32)
        onehot = sb("onehot", [P, TPP, TOPK, EXPERTS])
        chosen = sb("chosen", [P, TPP, EXPERTS], BF16)
        count = sb("count", [P, EXPERTS])
        row_of = sb("row_of", [P, TPP, EXPERTS])
        picked = sb("picked", [P, TPP, TOPK, EXPERTS])
        rows = sb("rows", [P, 2, TPP, TOPK], I32)

        cnt_i = sb("cnt_i", [P, 2, EXPERTS], I32)
        nblk = sb("nblk", [P, EXPERTS])
        last_blk = sb("last_blk", [P, EXPERTS])
        past = sb("past", [P, 2, EXPERTS])
        blk = sb("blk", [P, 8])
        tab = sb("tab", [1, P], I32)
        fill_row = sb("fill_row", [P, EXPERTS], I32)

        xb = sb("xb", [P, IN_RING, TPB, RW])
        w2 = sb("w2", [P, EXPERTS, FC * D])
        wb = sb("wb", [P, IN_RING, W2])
        xbT = sb("xbT", [P, RING, BT])
        hid = sb("hid", [P, RING, FC, BT])
        yb = sb("yb", [P, RING, TPB, D])
        x_first = sb("x_first", [P, RING, TPB, D])
        y_row = sb("y_row", [P, RING, TPB], I32)

        got = sb("got", [P, CRING, GT, TOPK, D])
        y = sb("y", [P, CRING, GT, D])
        st3 = sb("st3", [P, CRING, GT, 6])
        mv3 = sb("mv3", [P, CRING, GT, 2])
        rs3 = sb("rs3", [P, CRING, 3, GT])
        z = sb("z", [P, CRING, GT, D])
        res = sb("res", [P, CRING, GT, D])

        psum = ctx.enter_context(nc.psum_tensor("psum", [P, 8, 512], F32))
        xT_ps, adjT_ps, h_ps, s1_ps, agg_ps, route_ps = (
            psum[:, 0, :], psum[:, 1:3, :], psum[:, 3, :], psum[:, 4, :], psum[:, 5:7, :], psum[:, 7, :])
        agg_v = agg_ps[:, :, 0:TPG * (D + 1)].rearrange("p g (t c) -> p g t c", c=D + 1)
        h_v = h_ps[:, 0:TPG * HA].rearrange("p (t c) -> p t c", c=HA)
        gate_v = route_ps[:, 0:TPP * EXPERTS].rearrange("p (t e) -> p t e", e=EXPERTS)
        rank_v = route_ps[:, TPP * EXPERTS:2 * TPP * EXPERTS].rearrange("p (t e) -> p t e", e=EXPERTS)
        total_v = route_ps[:, 2 * TPP * EXPERTS:(2 * TPP + 1) * EXPERTS]

        weights_in, consts_in, late_in, w2_in = (
            sem("weights_in"), sem("consts_in"), sem("late_in"), sem("w2_in"))
        const_done = sem("const_done")
        pool_step, dve_step = sem("pool_step"), sem("dve_step")
        setup_pe, setup_dve = sem("setup_pe"), sem("setup_dve")
        x_in = [sem(f"x_in{c}") for c in range(len(XCHUNKS))]
        adj_in_s = [sem(f"adj_in{p}") for p in range(2)]
        stats1, rstd1_done, xn_done = sem("stats1"), sem("rstd1_done"), sem("xn_done")
        xT_done, xT_copied = sem("xT_done"), sem("xT_copied")
        adjT_g, h_g, s1_done, h_sb_g, sig_g, att_g = (
            sem("adjT_g"), sem("h_g"), sem("s1_done"), sem("h_sb_g"), sem("sig_g"), sem("att_g"))
        agg_g, xmid_done = sem("agg_g"), sem("xmid_done")
        rstd2_done, xn2_done, xrow_done = sem("rstd2_done"), sem("xn2_done"), sem("xrow_done")
        x_kept = sem("x_kept")
        x2T_done, x2T_copied, gate_done = sem("x2T_done"), sem("x2T_copied"), sem("gate_done")
        chosen_done, rank_done, ranks_used, rows_done = (
            sem("chosen_done"), sem("rank_done"), sem("ranks_used"), sem("rows_done"))
        scattered = [sem(f"scattered{p}") for p in range(2)]
        fill_done, table_cols, table_ps, table_done, filled = (
            sem("fill_done"), sem("table_cols"), sem("table_ps"), sem("table_done"), sem("filled"))
        block_in = [sem(f"block_in{q}") for q in range(IN_RING)]
        xbT_ps_done, xbT_done, l1_done, hid_done, first_done, l2_done, yb_done = (
            sem("xbT_ps_done"), sem("xbT_done"), sem("l1_done"), sem("hid_done"), sem("first_done"), sem("l2_done"), sem("yb_done"))
        yb_out = [sem(f"yb_out{q}") for q in range(RING)]
        got_in = [sem(f"got_in{q}") for q in range(CRING)]
        added, y_done, std_done, shift_done, z_done, scaled, res_done = (
            sem("added"), sem("y_done"), sem("std_done"), sem("shift_done"), sem("z_done"), sem("scaled"), sem("res_done"))
        dve_added = sem("dve_added")
        res_out = [sem(f"res_out{q}") for q in range(CRING)]
        pool_passed, dve_passed, sp_passed = sem("pool_passed"), sem("dve_passed"), sem("sp_passed")

        def free_after(i, slot):
            return 16 * SCATTERS * ((i - slot) // 2)

        x_v = x.rearrange("g (t p) c -> p (g t) c", p=P)
        out_v = out.rearrange("g (t p) c -> p (g t) c", p=P)
        adj_v = adj.rearrange("g (t p) n -> g p t n", p=P)
        token_v = token_y.rearrange("(t p k) c -> p t k c", p=P, k=TOPK)
        block = ctx.enter_context(nc.Block())

        @block.sync
        def _(sp):
            for dst, src in ((w_raw[:, :], gnn_w), (vec[:, 0:1], gnn_a1.rearrange("(p a) -> p a", a=1)),
                             (vec[:, 1:2], gnn_a2.rearrange("(p a) -> p a", a=1)),
                             (vec[:, 2:3], gnn_b.rearrange("(p a) -> p a", a=1)),
                             (h_bias[:, 0:D], gnn_b.rearrange("(a c) -> a c", a=1)),
                             (att_b_sb[:, :], att_b.rearrange("(a c) -> a c", a=1))):
                sp.dma_start(dst, src).then_inc(weights_in, 16)
            sp.dma_start(mask_rows[:, :], nodemask.rearrange("g (t p) -> (g t) p", p=P)).then_inc(consts_in, 16)

            def load_adj(i):
                for p in range(2):
                    if begun(i):
                        sp.wait_ge(adjT_g, 2 * i + p - 1)
                    sp.dma_start(adj_in[:, p, :, :], adj_v[2 * i + p, :, :, :]).then_inc(adj_in_s[p], 16)

            def load_w2(e):
                sp.dma_start(w2[:, bass.ds(e, 1), :], experts[bass.ds(e, 1), :, W2:WCOLS].rearrange("a p c -> p a c")
                             ).then_inc(w2_in, 16)

            load_adj(0)
            for dst, src in ((gate_w_sb[:, :], gate_w), (gate_b_bc[:, :], gate_b.partition_broadcast(P)),
                             (gamma_bc[:, :], gamma.partition_broadcast(P)),
                             (beta_bc[:, :], beta.partition_broadcast(P))):
                sp.dma_start(dst, src).then_inc(late_in, 16)
            load_w2(0)
            with sp.Fori(1, PAIRS) as i:
                load_adj(i)
                load_w2(i)

            sp.dma_start(sorted_x[PAD_ROW:PAD_ROW + BT, :].rearrange("(p t) c -> p t c", t=TPB),
                         pad_rows[:, :, :]).then_inc(filled, 16)
            sp.wait_ge(fill_done, 1)
            for e in range(0, EXPERTS, 2):
                row = sp.value_load(fill_row[0:1, e:e + 1], min_val=0, max_val=PAD_ROW - BT)
                sp.dma_start(sorted_x[bass.ds(row, BT), :].rearrange("(p t) c -> p t c", t=TPB),
                             pad_rows[:, :, :]).then_inc(filled, 16)
            sp.wait_ge(table_done, 1)

            def load_block(k, q):
                b = k * IN_RING + q
                entry = sp.value_load(tab[0:1, bass.ds(b, 1)], min_val=0, max_val=PAD_ROW * EXPERTS + EXPERTS - 1)
                e = (entry & (EXPERTS - 1)).with_bounds(min_val=0, max_val=EXPERTS - 1)
                row = (entry >> (EXPERTS.bit_length() - 1)).with_bounds(min_val=0, max_val=PAD_ROW)
                if begun(k):
                    sp.wait_ge(yb_done, b - IN_RING + 1)
                    sp.sem_inc(sp_passed, 1)
                sp.dma_start(wb[:, q, :], experts[bass.ds(e, 1), :, 0:W2].rearrange("a p c -> p (a c)")
                             ).then_inc(block_in[q], 16)
                if not begun(k) and q == 0:
                    sp.wait_ge(filled, 16 * (EXPERTS + 1))
                    sp.wait_ge(scattered[0], 16 * SCATTERS * PAIRS // 2)
                    sp.wait_ge(scattered[1], 16 * SCATTERS * PAIRS // 2)
                sp.dma_start(xb[:, q, :, :], sorted_x[bass.ds(row, BT), :].rearrange("(p t) c -> p t c", t=TPB)
                             ).then_inc(block_in[q], 16)

            for q in range(IN_RING):
                load_block(0, q)
            with sp.Fori(1, BTURNS) as k:
                for q in range(IN_RING):
                    load_block(k, q)

            for q in range(RING):
                sp.wait_ge(yb_out[q], 16 * TPB * NBLK // RING)

            def load_group(k, q):
                g = k * CRING + q
                if begun(k):
                    sp.wait_ge(added, g - CRING + 1)
                sp.dma_start(got[:, q, :, :, :], token_v[:, bass.ds(g * GT, GT), :, :]).then_inc(got_in[q], 16)

            for q in range(CRING):
                load_group(0, q)
            with sp.Fori(1, CTURNS) as k:
                for q in range(CRING):
                    load_group(k, q)
            for q in range(CRING):
                sp.wait_ge(res_out[q], 16 * CTURNS)

        @block.gpsimd
        def _(pool):
            g = nc.gpsimd
            g.memset(ident[:, :], 0.0).then_inc(pool_step, 1)
            g.memset(before[:, :], 1.0).then_inc(pool_step, 1)
            g.memset(pad_rows[:, :, :], 0.0).then_inc(pool_step, 1)
            g.memset(ones[:, :], 1.0).then_inc(const_done, 1)
            g.memset(ones_f[:, :], 1.0).then_inc(const_done, 1)
            g.memset(neg_half[:, :], -0.5).then_inc(const_done, 1)
            g.memset(eps_t[:, :], EPS).then_inc(const_done, 1)
            for k in range(TOPK):
                g.memset(xrow[:, :, k, :, FIRST], 1.0 - k).then_inc(const_done, 1)
            pool.wait_ge(pool_step, 3)
            g.affine_select(out=ident[:, :], in_=ident[:, :], compare_op=ALU.not_equal, fill=1.0, base=0,
                            pattern=[[-1, P]], channel_multiplier=1).then_inc(const_done, 1)
            g.affine_select(out=before[:, :], in_=before[:, :], compare_op=ALU.is_gt, fill=0.0, base=0,
                            pattern=[[1, P]], channel_multiplier=-1).then_inc(const_done, 1)
            for dst, pattern, base, by_partition in (
                    (iota_e[:, :], [[1, EXPERTS]], 0, 0), (iota_p[:, :], [[0, 1]], 0, 1),
                    (first_row[:, :], [[CAP, EXPERTS]], 0, 0), (result_row[:, :, :], [[1, TOPK], [2 * P, TILES]], 0, 2),
                    (pad_rows[:, :, TO], [[2, TPB]], 2 * TOKENS, 2 * TPB)):
                g.iota(dst, pattern=pattern, base=base, channel_multiplier=by_partition,
                       allow_small_or_imprecise_dtypes=True).then_inc(const_done, 1)

            def rstd1_of(c):
                lo, hi = XCHUNKS[c]
                pool.wait_ge(stats1, c + 1)
                g.tensor_scalar(rs1[:, lo:hi], mv1[:, lo:hi, 1], EPS, None, ALU.add).then_inc(pool_step, 1)
                g.tensor_scalar(shift1[:, 0, lo:hi], mv1[:, lo:hi, 0], -1.0, None, ALU.mult).then_inc(pool_step, 1)
                pool.wait_ge(pool_step, 3 + 3 * c + 2)
                g.tensor_tensor(rstd1[:, lo:hi], rs1[:, lo:hi], neg_half[:, 0:hi - lo], ALU.pow).then_inc(pool_step, 1)
                pool.wait_ge(pool_step, 3 + 3 * c + 3)
                g.tensor_tensor(shift1[:, 1, lo:hi], shift1[:, 0, lo:hi], rstd1[:, lo:hi], ALU.mult
                                ).then_inc(rstd1_done, (hi - lo) // TPP)

            def scatter(slot):
                for t in range(TPP):
                    for k in range(TOPK):
                        pool.indirect_dma_start(
                            sorted_x, bass.IndirectOffsetOnAxis(ap=rows[:, slot, t, k:k + 1], axis=0),
                            xrow[:, slot, k, t, :], None).then_inc(scattered[slot], 16)

            def turn(i, slot):
                pool.wait_ge(xrow_done, i + 1)
                pool.wait_ge(rows_done, i + 1)
                pool.sem_inc(pool_passed, 1)
                scatter(slot)

            for c in range(len(XCHUNKS)):
                rstd1_of(c)
            with pool.Fori(0, PAIRS // 2) as j:
                for s in range(2):
                    turn(2 * j + s, s)

            with pool.Fori(0, NBLK // RING) as k:
                for q in range(RING):
                    pool.wait_ge(yb_done, k * RING + q + 1)
                    pool.sem_inc(pool_passed, 1)
                    for t in range(TPB):
                        pool.indirect_dma_start(
                            token_y, bass.IndirectOffsetOnAxis(ap=y_row[:, q, t:t + 1], axis=0), yb[:, q, t, :], None,
                            bounds_check=TOKENS * TOPK - 1, oob_is_err=False).then_inc(yb_out[q], 16)

            def finish(k, q):
                i = k * CRING + q
                pool.wait_ge(z_done, i + 1)
                g.tensor_tensor(z[:, q, :, :], z[:, q, :, :], gamma_bc[:, None, :].broadcast_to([P, GT, D]), ALU.mult
                                ).then_inc(scaled, 1)
                if begun(k):
                    pool.wait_ge(res_out[q], 16 * k)
                pool.wait_ge(scaled, i + 1)
                g.tensor_tensor(res[:, q, 0:DVE_FROM, :], z[:, q, 0:DVE_FROM, :], xmid[:, bass.ds(i * GT, DVE_FROM), :],
                                ALU.add).then_inc(res_done, 1)

            for q in range(CRING):
                finish(0, q)
            with pool.Fori(1, CTURNS) as k:
                for q in range(CRING):
                    finish(k, q)

        @block.scalar
        def _(act):
            def load_x(c):
                lo, hi = XCHUNKS[c]
                act.dma_start(xmid[:, lo:hi, :], x_v[:, lo:hi, :]).then_inc(x_in[c], 16)

            load_x(0)
            act.wait_ge(weights_in, 16 * 6)
            load_x(1)

            def norm1(i):
                act.wait_ge(rstd1_done, i + 1)
                if begun(i):
                    act.wait_ge(xT_done, i)
                for t in range(TPP):
                    tile = bass.ds(i * TPP + t, 1)
                    last = act.activation(xn[:, t, :], xmid[:, tile, :].rearrange("p a c -> p (a c)"), ACT.Identity,
                                          bias=shift1[:, 1, tile], scale=rstd1[:, tile])
                last.then_inc(xn_done, 1)

            def transposed2(i):
                act.wait_ge(x2T_done, i + 1)
                if begun(i):
                    act.wait_ge(gate_done, i)
                act.copy(xn2T[:, :], xT_ps).then_inc(x2T_copied, 1)

            def keep(i, slot):
                if begun(i, 2):
                    act.wait_ge(scattered[slot], free_after(i, slot))
                act.copy(xrow[:, slot, :, :, TO], result_row[:, :, bass.ds(i * TPP, TPP)])
                act.copy(xrow[:, slot, :, :, 0:D], xn2[:, None, :, :].broadcast_to([P, TOPK, TPP, D])).then_inc(x_kept, 1)

            def weigh(i, slot):
                act.wait_ge(chosen_done, i + 1)
                for k in range(TOPK):
                    last = act.activation(xrow[:, slot, k, :, WEIGHT], lead[:, :], ACT.Sigmoid, scale=1.0 - 2.0 * k)
                last.then_inc(xrow_done, 1)

            def transposed(i):
                act.wait_ge(xT_done, i + 1)
                if begun(i):
                    act.wait_ge(h_g, 2 * i)
                act.copy(xnT[:, :], xT_ps).then_inc(xT_copied, 1)

            def keep_h(i, p, slot):
                act.wait_ge(h_g, 2 * i + p + 1)
                if begun(i, 2):
                    act.wait_ge(agg_g, 2 * i + p - 3)
                act.copy(h_sb[:, slot, p, :, :], h_v).then_inc(h_sb_g, 1)

            def sigmoids(i, slot):
                act.wait_ge(s1_done, i + 1)
                for p in range(2):
                    act.wait_ge(h_sb_g, 2 * i + p + 1)
                    if begun(i):
                        act.wait_ge(att_g, 2 * i + p - 1)
                    for t in range(TPG):
                        last = act.activation(sig[:, p, t, :], s1_ps[:, p * NODES:(p + 1) * NODES], ACT.Sigmoid,
                                              bias=h_sb[:, slot, p, t, HA - 1:HA])
                    last.then_inc(sig_g, 1)

            def norm2(i):
                act.wait_ge(rstd2_done, i + 1)
                if begun(i):
                    act.wait_ge(x2T_done, i)
                    act.wait_ge(x_kept, i)
                for t in range(TPP):
                    last = act.activation(xn2[:, t, :], xmid[:, bass.ds(i * TPP + t, 1), :].rearrange("p a c -> p (a c)"),
                                          ACT.Identity, bias=rs2[:, 1, t:t + 1], scale=rs2[:, 0, t:t + 1])
                last.then_inc(xn2_done, 1)

            def turn(m, slot):
                if valid(m + 1):
                    keep_h(m + 1, 0, 1 - slot)
                if valid(m - 2):
                    transposed2(m - 2)
                if valid(m + 2):
                    norm1(m + 2)
                if valid(m + 1):
                    keep_h(m + 1, 1, 1 - slot)
                    sigmoids(m + 1, 1 - slot)
                if valid(m + 2):
                    transposed(m + 2)
                if valid(m - 2):
                    keep(m - 2, slot)
                if valid(m - 1):
                    norm2(m - 1)
                if valid(m - 2):
                    weigh(m - 2, slot)

            act.wait_ge(const_done, 13)
            norm1(0)
            for c in range(2, len(XCHUNKS)):
                load_x(c)
            transposed(0)
            for m in range(-1, LOOP_FROM):
                turn(m, m % 2)
            with act.Fori(0, (LOOP_TO - LOOP_FROM) // 2) as j:
                for s in range(2):
                    turn(LOOP_FROM + 2 * j + s, (LOOP_FROM + s) % 2)
            for m in range(LOOP_TO, PAIRS + 2):
                turn(m, m % 2)

            act.wait_ge(fill_done, 1)
            for e in range(1, EXPERTS, 2):
                row = act.value_load(fill_row[0:1, e:e + 1], min_val=0, max_val=PAD_ROW - BT)
                act.dma_start(sorted_x[bass.ds(row, BT), :].rearrange("(p t) c -> p t c", t=TPB),
                              pad_rows[:, :, :]).then_inc(filled, 16)

            def relu(k, q):
                b = k * IN_RING + q
                act.wait_ge(l1_done, b + 1)
                if begun(k) or q >= RING:
                    act.wait_ge(l2_done, b - RING + 1)
                for c in range(FC):
                    last = act.activation(hid[:, q % RING, c, :], psum[:, 2 + q % 2, c * BT:(c + 1) * BT], ACT.Relu,
                                          bias=wb[:, q, B1 + c:B1 + c + 1])
                last.then_inc(hid_done, 1)
                if begun(k) or q >= RING:
                    act.wait_ge(yb_done, b - RING + 1)
                for t in range(TPB):
                    last = act.activation(x_first[:, q % RING, t, :], xb[:, q, t, 0:D], ACT.Identity,
                                          scale=xb[:, q, t, FIRST:FIRST + 1])
                last.then_inc(first_done, 1)

            for q in range(IN_RING):
                relu(0, q)
            with act.Fori(1, BTURNS) as k:
                for q in range(IN_RING):
                    relu(k, q)

            def deviation(k, q):
                act.wait_ge(y_done, k * CRING + q + 1)
                act.activation(rs3[:, q, 0, :], mv3[:, q, :, 1], ACT.Sqrt, bias=eps_t[:, :]).then_inc(std_done, 1)

            def normalise(k, q):
                g = k * CRING + q
                act.wait_ge(shift_done, g + 1)
                if begun(k):
                    act.wait_ge(res_done, g - CRING + 1)
                    act.wait_ge(dve_added, g - CRING + 1)
                for t in range(GT):
                    last = act.activation(z[:, q, t, :], y[:, q, t, :], ACT.Identity, bias=rs3[:, q, 2, t:t + 1],
                                          scale=rs3[:, q, 1, t:t + 1])
                last.then_inc(z_done, 1)

            def store_group(k, q):
                g = k * CRING + q
                act.wait_ge(res_done, g + 1)
                act.wait_ge(dve_added, g + 1)
                act.dma_start(out_v[:, bass.ds(g * GT, GT), :], res[:, q, :, :]).then_inc(res_out[q], 16)

            for q in range(CRING):
                deviation(0, q)
                normalise(0, q)
            store_group(0, 0)
            with act.Fori(1, CTURNS) as k:
                for q in range(CRING):
                    deviation(k, q)
                    normalise(k, q)
                    if q < CRING - 1:
                        store_group(k - 1, q + 1)
                    else:
                        store_group(k, 0)
            for q in range(1, CRING):
                store_group(CTURNS - 1, q)

        @block.vector
        def _(dve):
            v = nc.vector
            steps = [0]

            def step(instruction):
                instruction.then_inc(dve_step, 1)
                steps[0] = steps[0] + 1
                return steps[0]

            def setup():
                dve.wait_ge(weights_in, 16 * 6)
                v.tensor_copy(a1_bc[:, :], vec[:, 0:1].broadcast_to([P, P])).then_inc(setup_dve, 1)
                v.tensor_tensor(vec[:, 3:4], vec[:, 0:1], vec[:, 1:2], ALU.add).then_inc(setup_dve, 1)
                v.memset(h_bias[:, D:D + 1], 1.0).then_inc(setup_dve, 1)
                v.memset(w_aug[:, D:D + 1], 0.0).then_inc(setup_dve, 1)
                dve.wait_ge(const_done, 13)
                step(v.tensor_copy(count[:, :], first_row[:, :]))
                dve.wait_ge(setup_pe, 1)
                n = step(v.tensor_copy(mask_t[:, :], psum[:, 1, 0:TILES]))
                v.tensor_copy(w_aug[:, 0:D], psum[:, 0, 0:P]).then_inc(setup_dve, 1)
                v.tensor_copy(w_aug[:, D + 1:D + 2], psum[:, 0, P:P + 1]).then_inc(setup_dve, 1)
                v.tensor_copy(u1_bc[:, :], psum[:, 0, 2 * P:3 * P]).then_inc(setup_dve, 1)
                v.tensor_tensor(h_bias[:, D + 1:D + 2], psum[0:1, 0, P + 1:P + 2], att_b_sb[:, :], ALU.add
                                ).then_inc(setup_dve, 1)
                dve.wait_ge(dve_step, n)
                step(v.tensor_tensor(mask_sq[:, :], mask_t[:, :], mask_t[:, :], ALU.mult))

            def stats_of(c):
                lo, hi = XCHUNKS[c]
                dve.wait_ge(x_in[c], 16)
                if c:
                    dve.wait_ge(stats1, c)
                for t in range(lo, hi):
                    n = step(v.bn_stats(st1[:, t - lo, :], xmid[:, t, :]))
                dve.wait_ge(dve_step, n)
                for t in range(lo, hi):
                    last = v.bn_aggr(mv1[:, t, :], st1[:, t - lo, :])
                last.then_inc(stats1, 1)

            def attend(i, p, t):
                if t == 0:
                    dve.wait_ge(adjT_g, 2 * i + p + 1)
                    dve.wait_ge(sig_g, 2 * i + p + 1)
                last = v.scalar_tensor_tensor(
                    out=att[:, p, t, :], in0=adjT_ps[:, p, t * NODES:(t + 1) * NODES],
                    scalar=mask_t[:, bass.ds((2 * i + p) * TPG + t, 1)], in1=sig[:, p, t, :], op0=ALU.mult, op1=ALU.mult)
                if t == TPG - 1:
                    last.then_inc(att_g, 1)

            def by_graph(cols, i):
                return cols[:, bass.ds(i * TPP, TPP)].rearrange("p (g t) -> p g t", t=TPG)

            def row_numbers(i):
                dve.wait_ge(rank_done, i + 1)
                return step(v.tensor_tensor(row_of[:, :, :], rank_v, count[:, None, :].broadcast_to([P, TPP, EXPERTS]),
                                            ALU.add))

            def pick(n):
                dve.wait_ge(dve_step, n)
                v.tensor_tensor(count[:, :], count[:, :], total_v, ALU.add).then_inc(ranks_used, 1)
                return step(v.tensor_tensor(picked[:, :, :, :], onehot[:, :, :, :],
                                            row_of[:, :, None, :].broadcast_to([P, TPP, TOPK, EXPERTS]), ALU.mult))

            def place(i, slot, n):
                if begun(i, 2):
                    dve.wait_ge(scattered[slot], free_after(i, slot))
                dve.wait_ge(dve_step, n)
                with nc.allow_low_precision(reason="whole numbers below 2**24 are summed in float32, then stored as int32"):
                    v.tensor_reduce(rows[:, slot, :, :], picked[:, :, :, :], axis=AX, op=ALU.add).then_inc(rows_done, 1)

            def residual_and_place(m, slot):
                i, res, put, now = m - 1, valid(m - 1), valid(m - 3), valid(m)
                if res:
                    dve.wait_ge(agg_g, 2 * i + 2)
                    n = step(v.tensor_tensor(den[:, 0, :, :], agg_v[:, :, :, D], by_graph(mask_t, i), ALU.mult))
                if res:
                    dve.wait_ge(dve_step, n)
                    n = step(v.tensor_scalar(den[:, 1, :, :], den[:, 0, :, :], 1e-8, None, ALU.add))
                if res:
                    dve.wait_ge(dve_step, n)
                    n = step(v.reciprocal(den[:, 2, :, :], den[:, 1, :, :]))
                if now:
                    attend(m, 0, 0)
                if res:
                    dve.wait_ge(dve_step, n)
                    n = step(v.tensor_tensor(den[:, 3, :, :], den[:, 2, :, :], by_graph(mask_sq, i), ALU.mult))
                if put:
                    r = row_numbers(m - 3)
                if res:
                    dve.wait_ge(dve_step, n)
                    for t in range(TPP):
                        row = xmid[:, bass.ds(i * TPP + t, 1), :].rearrange("p a c -> p (a c)")
                        ins = v.scalar_tensor_tensor(out=row, in0=agg_v[:, t // TPG, t % TPG, 0:D],
                                                     scalar=den[:, 3, t // TPG, t % TPG:t % TPG + 1],
                                                     in1=row, op0=ALU.mult, op1=ALU.add)
                    ins.then_inc(xmid_done, 1)
                if put:
                    r = pick(r)
                if now:
                    attend(m, 0, 1)
                if put:
                    place(m - 3, slot, r)

            def variance_and_attention(m):
                i, var, now, n = m - 1, valid(m - 1), valid(m), None
                if var:
                    dve.wait_ge(xmid_done, i + 1)
                    dve.sem_inc(dve_passed, 1)
                    for t in range(TPP):
                        n = step(v.bn_stats(st2[:, t, :], xmid[:, bass.ds(i * TPP + t, 1), :].rearrange("p a c -> p (a c)")))
                if now:
                    attend(m, 1, 0)
                if var:
                    dve.wait_ge(dve_step, n)
                    dve.sem_inc(dve_passed, 1)
                    for t in range(TPP):
                        n = step(v.bn_aggr(mv2[:, t, :], st2[:, t, :]))
                if now:
                    attend(m, 1, 1)
                if var:
                    dve.wait_ge(dve_step, n)
                    n = step(v.tensor_scalar(var_eps[:, 0, :], mv2[:, :, 1], EPS, None, ALU.add))
                    step(v.tensor_scalar(var_eps[:, 1, :], mv2[:, :, 1], EPS, -0.5, ALU.add, ALU.mult))
                return n

            def half_bits(n):
                dve.wait_ge(dve_step, n)
                return step(v.tensor_scalar(bits[:, 0, :], var_eps[:, 0, :].bitcast(I32), 1, None, ALU.arith_shift_right))

            def first_guess(n):
                dve.wait_ge(dve_step, n)
                return step(v.tensor_scalar(bits[:, 1, :], bits[:, 0, :], -1.0, float(RSQRT_BITS), ALU.mult, ALU.add))

            guesses = [bits[:, 1, :].bitcast(F32), newton[:, 2, :], newton[:, 3, :], rs2[:, 0, :]]

            def square(k, n):
                dve.wait_ge(dve_step, n)
                return step(v.tensor_tensor(newton[:, 0, :], guesses[k], guesses[k], ALU.mult))

            def times_variance(n):
                dve.wait_ge(dve_step, n)
                return step(v.tensor_tensor(newton[:, 1, :], newton[:, 0, :], var_eps[:, 1, :], ALU.mult))

            def better_guess(k, n):
                dve.wait_ge(dve_step, n)
                return step(v.scalar_tensor_tensor(out=guesses[k + 1], in0=newton[:, 1, :], scalar=1.5, in1=guesses[k],
                                                   op0=ALU.add, op1=ALU.mult))

            def shift2(n):
                dve.wait_ge(dve_step, n)
                v.scalar_tensor_tensor(out=rs2[:, 1, :], in0=mv2[:, :, 0], scalar=-1.0, in1=rs2[:, 0, :],
                                       op0=ALU.mult, op1=ALU.mult).then_inc(rstd2_done, 1)

            def gate_logits(i):
                dve.wait_ge(gate_done, i + 1)
                n = step(v.tensor_tensor(logits[:, :, :], gate_v, gate_b_bc[:, None, :].broadcast_to([P, TPP, EXPERTS]),
                                         ALU.add))
                return n

            def largest(n):
                dve.wait_ge(dve_step, n)
                dve.sem_inc(dve_passed, 1)
                for t in range(TPP):
                    n = step(v.max(m8[:, t, :], logits[:, t, :]))
                return n

            def which(i, n):
                dve.wait_ge(dve_step, n)
                dve.sem_inc(dve_passed, 1)
                for t in range(TPP):
                    n = step(v.max_index(i8[:, t, :], m8[:, t, :], logits[:, t, :]))
                if begun(i):
                    dve.wait_ge(xrow_done, i)
                v.tensor_tensor(lead[:, :], m8[:, :, 0], m8[:, :, 1], ALU.subtract)
                return n

            def one_hot(n):
                dve.wait_ge(dve_step, n)
                return step(v.tensor_tensor(
                    onehot[:, :, :, :],
                    i8[:, :, 0:TOPK].rearrange("p t (k a) -> p t k a", a=1).broadcast_to([P, TPP, TOPK, EXPERTS]),
                    iota_e[:, None, None, :].broadcast_to([P, TPP, TOPK, EXPERTS]), ALU.is_equal))

            def choose(n):
                dve.wait_ge(dve_step, n)
                v.tensor_tensor(chosen[:, :, :], onehot[:, :, 0, :], onehot[:, :, 1, :], ALU.add).then_inc(chosen_done, 1)

            def norm_and_route(m, r):
                var, now = valid(m - 1), valid(m - 2)
                if var:
                    r = half_bits(r)
                if now:
                    n = gate_logits(m - 2)
                if var:
                    r = first_guess(r)
                if now:
                    n = largest(n)
                if var:
                    r = square(0, r)
                if now:
                    n = which(m - 2, n)
                if var:
                    r = times_variance(r)
                    r = better_guess(0, r)
                if now:
                    n = one_hot(n)
                if var:
                    r = square(1, r)
                    r = times_variance(r)
                if now:
                    choose(n)
                if var:
                    r = better_guess(1, r)
                    r = square(2, r)
                    r = times_variance(r)
                    r = better_guess(2, r)
                    shift2(r)

            def turn(m, slot):
                residual_and_place(m, 1 - slot)
                norm_and_route(m, variance_and_attention(m))

            stats_of(0)
            setup()
            for c in range(1, len(XCHUNKS) - 1):
                stats_of(c)
            turn(0, 0)
            stats_of(len(XCHUNKS) - 1)
            turn(1, 1)
            turn(2, 0)
            per = steps[0]
            turn(3, 1)
            per = steps[0] - per
            base = steps[0]
            with dve.Fori(0, (LOOP_TO - LOOP_FROM) // 2) as j:
                for s in range(2):
                    steps[0] = base + j * (2 * per) + s * per
                    turn(LOOP_FROM + 2 * j + s, (LOOP_FROM + s) % 2)
            steps[0] = base + per * (LOOP_TO - LOOP_FROM)
            for m in range(LOOP_TO, PAIRS + 3):
                turn(m, m % 2)

            dve.wait_ge(dve_step, steps[0])
            v.tensor_copy(fill_row[:, :], count[:, :]).then_inc(fill_done, 1)
            n = step(v.scalar_tensor_tensor(out=past[:, 0, :], in0=count[:, :], scalar=float(BT - 1), in1=first_row[:, :],
                                            op0=ALU.add, op1=ALU.subtract))
            dve.wait_ge(dve_step, n)
            n = step(v.tensor_copy(cnt_i[:, 0, :], past[:, 0, :]))
            dve.wait_ge(dve_step, n)
            n = step(v.tensor_scalar(cnt_i[:, 1, :], cnt_i[:, 0, :], BT.bit_length() - 1, None, ALU.arith_shift_right))
            dve.wait_ge(dve_step, n)
            n = step(v.tensor_copy(nblk[:, :], cnt_i[:, 1, :]))
            dve.wait_ge(dve_step, n)
            n = step(v.tensor_tensor_scan(last_blk[:, :], ones_f[:, 0:EXPERTS], nblk[:, :], 0.0, ALU.mult, ALU.add))
            dve.wait_ge(dve_step, n)
            n = step(v.tensor_scalar(past[:, 0, :], last_blk[:, :], iota_p[:, :], None, ALU.is_le))
            dve.wait_ge(dve_step, n)
            step(v.tensor_reduce(blk[:, 0:1], past[:, 0, :], axis=AX, op=ALU.add))
            n = step(v.tensor_tensor(past[:, 1, :], past[:, 0, :], nblk[:, :], ALU.mult))
            dve.wait_ge(dve_step, n)
            n = step(v.tensor_reduce(blk[:, 1:2], past[:, 1, :], axis=AX, op=ALU.add))
            dve.wait_ge(dve_step, n)
            step(v.tensor_scalar(blk[:, 3:4], blk[:, 0:1], float(EXPERTS - 1), None, ALU.min))
            step(v.tensor_scalar(blk[:, 4:5], blk[:, 0:1], float(EXPERTS), None, ALU.is_lt))
            n = step(v.tensor_tensor(blk[:, 2:3], iota_p[:, :], blk[:, 1:2], ALU.subtract))
            dve.wait_ge(dve_step, n)
            n = step(v.scalar_tensor_tensor(out=blk[:, 5:6], in0=blk[:, 2:3], scalar=float(BT), in1=blk[:, 4:5],
                                            op0=ALU.mult, op1=ALU.mult))
            dve.wait_ge(dve_step, n)
            n = step(v.scalar_tensor_tensor(out=blk[:, 6:7], in0=blk[:, 0:1], scalar=float(CAP), in1=blk[:, 5:6],
                                            op0=ALU.mult, op1=ALU.add))
            dve.wait_ge(dve_step, n)
            v.scalar_tensor_tensor(out=blk[:, 7:8], in0=blk[:, 6:7], scalar=float(EXPERTS), in1=blk[:, 3:4],
                                   op0=ALU.mult, op1=ALU.add).then_inc(table_cols, 1)
            dve.wait_ge(table_ps, 1)
            v.tensor_copy(tab[:, :], psum[0:1, 0, 0:P]).then_inc(table_done, 1)

            def block_x(k, q):
                b, h = k * IN_RING + q, q % RING
                dve.wait_ge(xbT_ps_done, b + 1)
                if begun(k) or q >= RING:
                    dve.wait_ge(l1_done, b - RING + 1)
                v.tensor_copy(xbT[:, h, :], psum[:, q % 2, 0:BT]).then_inc(xbT_done, 1)

            def block_y(b, q, earlier):
                h = q % RING
                if begun(earlier):
                    dve.wait_ge(yb_out[h], 16 * TPB * earlier)
                dve.wait_ge(l2_done, b + 1)
                n = step(v.tensor_tensor(
                    yb[:, h, :, :], psum[:, 4 + q % 2, 0:TPB * D].rearrange("p (t c) -> p t c", c=D),
                    wb[:, q, None, B2:B2 + D].broadcast_to([P, TPB, D]), ALU.add))
                v.tensor_copy(y_row[:, h, :], xb[:, q, :, TO])
                dve.wait_ge(first_done, b + 1)
                dve.wait_ge(dve_step, n)
                for t in range(TPB):
                    last = v.scalar_tensor_tensor(out=yb[:, h, t, :], in0=yb[:, h, t, :],
                                                  scalar=xb[:, q, t, WEIGHT:WEIGHT + 1],
                                                  in1=x_first[:, h, t, :], op0=ALU.mult, op1=ALU.add)
                last.then_inc(yb_done, 1)

            def add_beta(k):
                tiles = xmid[:, bass.ds(k * GT, GT), :]
                v.tensor_tensor(tiles, tiles, beta_bc[:, None, :].broadcast_to([P, GT, D]), ALU.add)

            base = steps[0]

            def turn_b(k, q):
                block_x(k, q)
                b = k * IN_RING + q - 2
                steps[0] = base + b
                block_y(b, (q - 2) % IN_RING, k * (IN_RING // RING) + (q - 2) // RING)

            block_x(0, 0)
            block_x(0, 1)
            for q in range(2, IN_RING):
                turn_b(0, q)
            with dve.Fori(1, 1 + GROUPS // 2) as k:
                for q in range(IN_RING):
                    turn_b(k, q)
                    if q % (IN_RING // 2) == 0:
                        add_beta(2 * (k - 1) + q // (IN_RING // 2))
            for k in range(1 + GROUPS // 2, BTURNS):
                for q in range(IN_RING):
                    turn_b(k, q)
            steps[0] = base + NBLK - 2
            for b in (NBLK - 2, NBLK - 1):
                block_y(b, b % IN_RING, b // RING)

            def add(k, q):
                dve.wait_ge(got_in[q], 16 * (k + 1))
                if begun(k):
                    dve.wait_ge(z_done, k * CRING + q - CRING + 1)
                v.tensor_tensor(y[:, q, :, :], got[:, q, :, 0, :], got[:, q, :, 1, :], ALU.add).then_inc(added, 1)

            def aggregate(q):
                for t in range(GT):
                    last = v.bn_aggr(mv3[:, q, t, :], st3[:, q, t, :])
                last.then_inc(y_done, 1)

            def stats(k, q):
                dve.wait_ge(added, k * CRING + q + 1)
                dve.sem_inc(dve_passed, 1)
                for t in range(GT):
                    step(v.bn_stats(st3[:, q, t, :], y[:, q, t, :]))

            def shift(g, q):
                dve.wait_ge(std_done, g + 1)
                n = step(v.reciprocal(rs3[:, q, 1, :], rs3[:, q, 0, :]))
                dve.wait_ge(dve_step, n)
                v.scalar_tensor_tensor(out=rs3[:, q, 2, :], in0=mv3[:, q, :, 0], scalar=-1.0, in1=rs3[:, q, 1, :],
                                       op0=ALU.mult, op1=ALU.mult).then_inc(shift_done, 1)

            def finish(k, q):
                g = k * CRING + q
                dve.wait_ge(scaled, g + 1)
                if begun(k):
                    dve.wait_ge(res_out[q], 16 * k)
                v.tensor_tensor(res[:, q, DVE_FROM:GT, :], z[:, q, DVE_FROM:GT, :],
                                xmid[:, bass.ds(g * GT + DVE_FROM, GT - DVE_FROM), :], ALU.add).then_inc(dve_added, 1)

            def turn_c(k, q):
                last_q = (q - 1) % CRING
                n = steps[0]
                add(k, q)
                dve.wait_ge(dve_step, n)
                dve.sem_inc(dve_passed, 1)
                aggregate(last_q)
                stats(k, q)
                shift(k * CRING + q - 1, last_q)

            add(0, 0)
            stats(0, 0)
            for q in range(1, CRING):
                turn_c(0, q)
            finish(0, 0)
            base, per = steps[0], GT + 1
            with dve.Fori(1, CTURNS) as k:
                for q in range(CRING):
                    steps[0] = base + ((k - 1) * CRING + q) * per
                    turn_c(k, q)
                    if q < CRING - 1:
                        finish(k - 1, q + 1)
                    else:
                        finish(k, 0)
            dve.wait_ge(dve_step, base + (GROUPS - CRING) * per)
            aggregate(CRING - 1)
            steps[0] = base + (GROUPS - CRING) * per
            shift(GROUPS - 1, CRING - 1)
            for q in range(1, CRING):
                finish(CTURNS - 1, q)

        @block.tensor
        def _(pe):
            mm, tr = nc.tensor.matmul, nc.tensor.transpose

            pe.wait_ge(const_done, 13)
            pe.wait_ge(setup_dve, 4)
            tr(psum[:, 0, 0:P], w_raw[:, :], ident[:, :])
            mm(psum[:, 0, P:P + 1], w_raw[:, :], vec[:, 1:2], start=True, stop=True)
            mm(psum[0:1, 0, P + 1:P + 2], vec[:, 2:3], vec[:, 3:4], start=True, stop=True)
            mm(psum[:, 0, 2 * P:3 * P], w_raw[:, :], a1_bc[:, :], start=True, stop=True)
            pe.wait_ge(consts_in, 16)
            tr(psum[:, 1, 0:TILES], mask_rows[:, :], ident[0:TILES, 0:TILES]).then_inc(setup_pe, 1)
            pe.wait_ge(setup_dve, 8)

            def transpose_x(i):
                pe.wait_ge(xn_done, i + 1)
                if begun(i, 4):
                    pe.wait_ge(x2T_copied, i - 3)
                for t in range(TPP):
                    last = tr(xT_ps[:, t * P:(t + 1) * P], xn[:, t, :], ident[:, :])
                last.then_inc(xT_done, 1)

            def transpose_adj(i):
                for p in range(2):
                    pe.wait_ge(adj_in_s[p], 16 * (i + 1))
                    if begun(i):
                        pe.wait_ge(att_g, 2 * i + p - 1)
                    for jt in range(TPG):
                        for it in range(TPG):
                            last = tr(adjT_ps[:, p, jt * NODES + it * P:jt * NODES + (it + 1) * P],
                                      adj_in[:, p, it, jt * P:(jt + 1) * P], ident[:, :])
                    last.then_inc(adjT_g, 1)

            def project(i, p):
                if p == 0:
                    pe.wait_ge(xT_copied, i + 1)
                if begun(i) or p:
                    pe.wait_ge(h_sb_g, 2 * i + p)
                for t in range(TPG):
                    c = (p * TPG + t) * P
                    mm(h_v[:, t, :], xnT[:, c:c + P], w_aug[:, :], start=True, stop=False)
                    last = mm(h_v[:, t, :], ones_f[0:1, :], h_bias[:, :], start=False, stop=True)
                last.then_inc(h_g, 1)

            def project_s1(i):
                if begun(i):
                    pe.wait_ge(sig_g, 2 * i)
                mm(s1_ps, u1_bc[:, :], xnT[:, :], start=True, stop=True).then_inc(s1_done, 1)

            def aggregate(i, slot):
                if begun(i):
                    pe.wait_ge(xmid_done, i)
                for p in range(2):
                    pe.wait_ge(h_sb_g, 2 * i + p + 1)
                    pe.wait_ge(att_g, 2 * i + p + 1)
                    for it in range(TPG):
                        for jt in range(TPG):
                            last = mm(agg_v[:, p, it, :], att[:, p, jt, it * P:(it + 1) * P], h_sb[:, slot, p, jt, 0:D + 1],
                                      start=(jt == 0), stop=(jt == TPG - 1))
                    last.then_inc(agg_g, 1)

            def transpose_x2(i, fronts):
                pe.wait_ge(xn2_done, i + 1)
                pe.wait_ge(xT_copied, fronts)
                for t in range(TPP):
                    last = tr(xT_ps[:, t * P:(t + 1) * P], xn2[:, t, :], ident[:, :])
                last.then_inc(x2T_done, 1)

            def gate(i):
                if not begun(i):
                    pe.wait_ge(late_in, 16 * 4)
                pe.wait_ge(x2T_copied, i + 1)
                if begun(i):
                    pe.wait_ge(ranks_used, i)
                for t in range(TPP):
                    last = mm(gate_v[:, t, :], xn2T[:, t * P:(t + 1) * P], gate_w_sb[:, :], start=True, stop=True)
                last.then_inc(gate_done, 1)

            def rank(i):
                pe.wait_ge(chosen_done, i + 1)
                for t in range(TPP):
                    for s in range(t):
                        mm(rank_v[:, t, :], ones[:, :], chosen[:, s, :], start=(s == 0), stop=False)
                    mm(rank_v[:, t, :], before[:, :], chosen[:, t, :], start=(t == 0), stop=True)
                for t in range(TPP):
                    last = mm(total_v, ones[:, :], chosen[:, t, :], start=(t == 0), stop=(t == TPP - 1))
                last.then_inc(rank_done, 1)

            def turn(m, slot):
                if valid(m + 1):
                    project(m + 1, 0)
                if valid(m):
                    transpose_adj(m)
                if valid(m - 3):
                    rank(m - 3)
                if valid(m - 2):
                    transpose_x2(m - 2, m + 2 if not isinstance(m, int) else min(m + 2, PAIRS))
                if valid(m + 1):
                    project_s1(m + 1)
                    project(m + 1, 1)
                if valid(m - 2):
                    gate(m - 2)
                if valid(m + 2):
                    transpose_x(m + 2)
                if valid(m):
                    aggregate(m, slot)

            transpose_x(0)
            for m in range(-1, LOOP_FROM):
                turn(m, m % 2)
            with pe.Fori(0, (LOOP_TO - LOOP_FROM) // 2) as j:
                for s in range(2):
                    turn(LOOP_FROM + 2 * j + s, (LOOP_FROM + s) % 2)
            for m in range(LOOP_TO, PAIRS + 3):
                turn(m, m % 2)

            pe.wait_ge(table_cols, 1)
            mm(psum[0:1, 0, 0:P], blk[:, 7:8], ident[:, :], start=True, stop=True).then_inc(table_ps, 1)
            pe.wait_ge(table_done, 1)

            def turn_x(k, q, early):
                pe.wait_ge(block_in[q], 32 * (k + 1))
                if not early:
                    pe.wait_ge(xbT_done, k * IN_RING + q - 1)
                for t in range(TPB):
                    last = tr(psum[:, q % 2, t * P:(t + 1) * P], xb[:, q, t, 0:D], ident[:, :])
                last.then_inc(xbT_ps_done, 1)

            def layer1(b, q, early):
                pe.wait_ge(xbT_done, b + 1)
                if not early:
                    pe.wait_ge(hid_done, b - 1)
                for c in range(FC):
                    last = mm(psum[:, 2 + q % 2, c * BT:(c + 1) * BT], wb[:, q, c * P:(c + 1) * P], xbT[:, q % RING, :],
                              start=True, stop=True)
                last.then_inc(l1_done, 1)

            def layer2(b, q, early, e):
                pe.wait_ge(hid_done, b + 1)
                if not early:
                    pe.wait_ge(yb_done, b - 1)
                for t in range(TPB):
                    for c in range(FC):
                        last = mm(psum[:, 4 + q % 2, t * D:(t + 1) * D], hid[:, q % RING, c, t * P:(t + 1) * P],
                                  w2[:, e, c * D:(c + 1) * D].rearrange("p a c -> p (a c)"), start=(c == 0), stop=(c == FC - 1))
                last.then_inc(l2_done, 1)

            def expert_of(b):
                entry = pe.value_load(tab[0:1, bass.ds(b, 1)], min_val=0, max_val=PAD_ROW * EXPERTS + EXPERTS - 1)
                return bass.ds((entry & (EXPERTS - 1)).with_bounds(min_val=0, max_val=EXPERTS - 1), 1)

            pe.wait_ge(w2_in, 16 * EXPERTS)
            for q in range(IN_RING):
                turn_x(0, q, q < 2)
                if q >= 1:
                    layer1(q - 1, q - 1, q - 1 < 2)
                if q >= 2:
                    layer2(q - 2, q - 2, q - 2 < 2, expert_of(q - 2))
            with pe.Fori(1, BTURNS) as k:
                for q in range(IN_RING):
                    b = k * IN_RING + q
                    turn_x(k, q, False)
                    e = expert_of(b - 2)
                    layer1(b - 1, (q - 1) % IN_RING, False)
                    layer2(b - 2, (q - 2) % IN_RING, False, e)
            layer1(NBLK - 1, IN_RING - 1, False)
            for b in (NBLK - 2, NBLK - 1):
                layer2(b, b % IN_RING, False, expert_of(b))


def kernel(x, adj, nodemask, L0_gnn_W, L0_gnn_b, L0_gnn_a1, L0_gnn_a2, L0_gnn_att_b, L0_ffn_gate_w, L0_ffn_gate_b,
           L0_ffn_w1, L0_ffn_b1, L0_ffn_w2, L0_ffn_b2, L0_ffn_gamma, L0_ffn_beta):
    import numpy as np
    import concourse.bacc as bacc
    from concourse.bass_utils import run_bass_kernel_spmd

    w1, w2 = np.asarray(L0_ffn_w1), np.asarray(L0_ffn_w2)
    b1, b2 = np.asarray(L0_ffn_b1), np.asarray(L0_ffn_b2)
    experts = np.concatenate([
        w1,
        b1.reshape(EXPERTS, FC, P).transpose(0, 2, 1),
        np.broadcast_to(b2[:, None, :], (EXPERTS, P, D)),
        w2.reshape(EXPERTS, FC, P, D).transpose(0, 2, 1, 3).reshape(EXPERTS, P, FC * D),
    ], axis=2)
    arrays = dict(
        x=x, adj=adj, nodemask=nodemask, gnn_w=L0_gnn_W, gnn_b=L0_gnn_b, gnn_a1=L0_gnn_a1, gnn_a2=L0_gnn_a2,
        att_b=np.asarray(L0_gnn_att_b).reshape(1), gate_w=L0_ffn_gate_w, gate_b=L0_ffn_gate_b, experts=experts,
        gamma=L0_ffn_gamma, beta=L0_ffn_beta)
    arrays = {f"{name}_dram": np.ascontiguousarray(a) for name, a in arrays.items()}
    nc = bacc.Bacc("TRN2", target_bir_lowering=False, num_devices=1)
    args = [nc.dram_tensor(name, a.shape, F32, kind="ExternalInput").ap() for name, a in arrays.items()]
    out = nc.dram_tensor("out_dram", (GRAPHS, NODES, D), F32, kind="ExternalOutput").ap()
    build(nc, *args, out)
    return run_bass_kernel_spmd(nc, [arrays], core_ids=[0]).results[0]["out_dram"]
```
